# Optimizing a Trainium2 kernel written in Bass

```python
import numpy as np
import jax
import jax.numpy as jnp

def _softmax(x, axis=-1):
    return jax.nn.softmax(x, axis=axis)
def _gelu(x):
    return jax.nn.gelu(x, approximate=True)
def _silu(x):
    return jax.nn.silu(x)
def _sigmoid(x):
    return jax.nn.sigmoid(x)
def _layernorm(x, axis=-1, eps=1e-5):
    m = jnp.mean(x, axis=axis, keepdims=True)
    v = jnp.var(x, axis=axis, keepdims=True)
    return (x - m) / jnp.sqrt(v + eps)
def _scatter_add(tgt, idx, src, axis=0):
    return tgt.at[idx].add(src)
def _segment_sum(src, seg, n):
    return jax.ops.segment_sum(src, seg, n)

kernel_name = 'mk_adj_preln_d2_adj_512_bb5bd6'

def setup_inputs(seed: int = 0):
    np.random.seed(seed)
    _w = jnp.asarray
    def _rec_inputs():
        import jax
        import jax.numpy as jnp
        _gk = jax.random.key(seed)
        x = 7.22e-05 + 1 * jax.random.normal(jax.random.fold_in(_gk, 1), (64, 256, 512), jnp.float32)
        _w = (1.0 + jnp.arange(256, dtype=jnp.float32)) ** -0.5
        _w = _w / _w.mean()
        _pij = jnp.clip(0.0625 * _w[:, None] * _w[None, :], 0.0, 1.0)
        _a = jax.random.uniform(jax.random.fold_in(_gk, 2), (64, 256, 256)) < _pij
        _a = jnp.logical_or(_a, jnp.swapaxes(_a, -1, -2))
        _a = jnp.logical_or(_a, jnp.eye(256, dtype=bool))
        _af = _a.astype(jnp.float32)
        _af = _af * jax.random.uniform(jax.random.fold_in(_gk, 3), (64, 256, 256), jnp.float32, 0.05, 1)
        adj = _af
        return x, adj
    x, adj = _rec_inputs()
    def _L0_gnn_setup():
        import jax, jax.numpy as jnp
        import numpy as np
        B, N, D = (8, 2048, 512)
        key = jax.random.key(seed)
        ks = jax.random.split(key, 8)
        scale = 0.5 / np.sqrt(D)
        x = jax.random.normal(ks[0], (B, N, D), dtype=jnp.float32)
        adj = jax.random.uniform(ks[1], (B, N, N), dtype=jnp.float32)
        Wq_w = jax.random.normal(ks[2], (D, D), dtype=jnp.float32) * scale
        Wk_w = jax.random.normal(ks[3], (D, D), dtype=jnp.float32) * scale
        Wv_w = jax.random.normal(ks[4], (D, D), dtype=jnp.float32) * scale
        Wq_b = jnp.zeros((D,), dtype=jnp.float32)
        Wk_b = jnp.zeros((D,), dtype=jnp.float32)
        Wv_b = jnp.zeros((D,), dtype=jnp.float32)
        return {'x': x, 'adj': adj, 'Wq_w': Wq_w, 'Wq_b': Wq_b, 'Wk_w': Wk_w, 'Wk_b': Wk_b, 'Wv_w': Wv_w, 'Wv_b': Wv_b}
    _L0_gnn_all = _L0_gnn_setup()
    _L0_gnn_in = {k: v for k, v in _L0_gnn_all.items() if k in ('Wq_w', 'Wq_b', 'Wk_w', 'Wk_b', 'Wv_w', 'Wv_b', )}
    del _L0_gnn_all

    def _L1_gnn_setup():
        import jax, jax.numpy as jnp
        import numpy as np
        B, N, F_IN, F_OUT = (8, 2048, 512, 512)
        key = jax.random.key(seed)
        k1, k2, k3, k4 = jax.random.split(key, 4)
        X = jax.random.normal(k1, (B, N, F_IN), dtype=jnp.float32)
        A = jax.random.uniform(k2, (B, N, N), dtype=jnp.float32)
        bound = 1.0 / np.sqrt(F_IN)
        W = jax.random.uniform(k3, (F_IN, F_OUT), dtype=jnp.float32, minval=-bound, maxval=bound)
        b = jax.random.uniform(k4, (F_OUT,), dtype=jnp.float32, minval=-bound, maxval=bound)
        return {'X': X, 'A': A, 'W': W, 'b': b}
    _L1_gnn_all = _L1_gnn_setup()
    _L1_gnn_in = {k: v for k, v in _L1_gnn_all.items() if k in ('W', 'b', )}
    del _L1_gnn_all

    return {
        "x": x,
        "adj": adj,
        "L0_gnn_Wq_w": _L0_gnn_in["Wq_w"],
        "L0_gnn_Wq_b": _L0_gnn_in["Wq_b"],
        "L0_gnn_Wk_w": _L0_gnn_in["Wk_w"],
        "L0_gnn_Wk_b": _L0_gnn_in["Wk_b"],
        "L0_gnn_Wv_w": _L0_gnn_in["Wv_w"],
        "L0_gnn_Wv_b": _L0_gnn_in["Wv_b"],
        "L1_gnn_W": _L1_gnn_in["W"],
        "L1_gnn_b": _L1_gnn_in["b"],
    }

def reference(x, adj, L0_gnn_Wq_w, L0_gnn_Wq_b, L0_gnn_Wk_w, L0_gnn_Wk_b, L0_gnn_Wv_w, L0_gnn_Wv_b, L1_gnn_W, L1_gnn_b):
    import jax
    import jax.numpy as jnp
    def _L0_gnn_ref(x, adj, Wq_w, Wq_b, Wk_w, Wk_b, Wv_w, Wv_b):
        import jax, jax.numpy as jnp
        import numpy as np
        B, N, D = (8, 2048, 512)
        query = jnp.einsum('bnd,od->bno', x, Wq_w) + Wq_b
        keyt = jnp.einsum('bnd,od->bno', x, Wk_w) + Wk_b
        value = jnp.einsum('bnd,od->bno', x, Wv_w) + Wv_b
        weight = jnp.einsum('bqd,bkd->bqk', query, keyt)
        weight = adj * jnp.exp(weight)
        weight = weight / jnp.sum(weight, axis=2, keepdims=True)
        return jnp.einsum('bqk,bkd->bqd', weight, value)

    def _L1_gnn_ref(X, A, W, b):
        import jax, jax.numpy as jnp
        import numpy as np
        B, N, F_IN, F_OUT = (8, 2048, 512, 512)
        A_hat = A + jnp.eye(A.shape[-1], dtype=A.dtype)
        d_inv_sqrt = A_hat.sum(axis=-1) ** (-0.5)
        L = A_hat * d_inv_sqrt[:, :, None] * d_inv_sqrt[:, None, :]
        x = X @ W + b
        return jnp.einsum('bij,bjf->bif', L, x)

    h = jnp.maximum(_layernorm(x, axis=-1), 0.0)
    x = x + _L0_gnn_ref(h, adj, L0_gnn_Wq_w, L0_gnn_Wq_b, L0_gnn_Wk_w, L0_gnn_Wk_b, L0_gnn_Wv_w, L0_gnn_Wv_b)
    h = jnp.maximum(_layernorm(x, axis=-1), 0.0)
    x = x + _L1_gnn_ref(h, adj, L1_gnn_W, L1_gnn_b)
    return x


_drawn_inputs = setup_inputs


def setup_inputs(seed=0):
    import zlib

    import numpy as np

    out = dict(_drawn_inputs(seed))
    spreads = {'L0_gnn_Wq_b': (0.0, 0.1), 'L0_gnn_Wk_b': (0.0, 0.1), 'L0_gnn_Wv_b': (0.0, 0.1)}
    factors = {}
    for name, (base, spread) in spreads.items():
        noise = np.random.default_rng([zlib.crc32(name.encode()), seed]).standard_normal(out[name].shape)
        drawn = base * np.exp(spread * noise) if base else spread * noise
        out[name] = jnp.asarray(drawn.astype(out[name].dtype))
    for name, factor in factors.items():
        out[name] = (out[name] * factor).astype(out[name].dtype)
    return out
```

```python
import concourse.bass as bass
from concourse import mybir
from contextlib import ExitStack

B, N, D = 64, 256, 512
P = 128
NT = N // P
DC = D // P
EPS = 1e-5


def gnn_program(nc, x, adj, wq, bq, wk, bk, wv, bv, w, b, out):
    fp32, f32r = mybir.dt.float32, mybir.dt.float32r
    ALU, ACT, AX = mybir.AluOpType, mybir.ActivationFunctionType, mybir.AxisListType

    ctx = ExitStack()
    with ctx:
        def sb(name, shape, dt=fp32):
            return ctx.enter_context(nc.sbuf_tensor(name, shape, dt))

        def sem(name):
            return ctx.enter_context(nc.semaphore(name))

        def sems(name, n=2):
            return [sem(f"{name}{k}") for k in range(n)]

        m_hi, m_lo = sb("m_hi", [P, DC, D], f32r), sb("m_lo", [P, DC, D], f32r)
        wvt_hi, wvt_lo = sb("wvt_hi", [P, DC, D], f32r), sb("wvt_lo", [P, DC, D], f32r)
        w_hi, w_lo = sb("w_hi", [P, DC, D], f32r), sb("w_lo", [P, DC, D], f32r)
        u_col = sb("u_col", [P, DC])
        c_row = sb("c_row", [P, D])
        bb_col = sb("bb_col", [P, 1])
        bv_row, b_row = sb("bv_row", [P, D]), sb("b_row", [P, D])
        ident = sb("ident", [P, P])
        eye = sb("eye", [P, NT, N])
        ones = sb("ones", [P, P])
        ones_r = sb("ones_r", [P, 2], f32r)
        minus_half = sb("minus_half", [P, NT])
        bq_col, bk_col = sb("bq_col", [P, DC]), sb("bk_col", [P, DC])
        bq_wide = sb("bq_wide", [P, DC, P])
        bv_in, b_in = sb("bv_in", [1, D]), sb("b_in", [1, D])

        x_in = sb("x_in", [P, NT, D])
        adj_in = sb("adj_in", [P, NT, N])
        h = sb("h", [P, NT, D])
        ht_hi, ht_lo = sb("ht_hi", [P, DC, N], f32r), sb("ht_lo", [P, DC, N], f32r)
        g_hi, g_lo = sb("g_hi", [P, DC, N], f32r), sb("g_lo", [P, DC, N], f32r)
        adjt = sb("adjt", [P, NT, N])
        e = sb("e", [P, NT, N])
        p = sb("p", [P, NT, N])
        p_hi, p_lo = sb("p_hi", [P, NT, N], f32r), sb("p_lo", [P, NT, N], f32r)
        v_hi, v_lo = sb("v_hi", [P, NT, D], f32r), sb("v_lo", [P, NT, D], f32r)
        xb = sb("xb", [P, NT, D])
        hat = sb("hat", [P, NT, N])
        hat_hi, hat_lo = sb("hat_hi", [P, NT, N], f32r), sb("hat_lo", [P, NT, N], f32r)
        h1_hi, h1_lo = sb("h1_hi", [P, NT, D], f32r), sb("h1_lo", [P, NT, D], f32r)
        z_hi, z_lo = sb("z_hi", [P, DC, N], f32r), sb("z_lo", [P, DC, N], f32r)
        late = sb("late", [P, 4, NT * D])
        wq_in = late[:, 0:2, :].rearrange("p a (c d) -> p (a c) d", d=D)
        wk_in = late[:, 2:4, :].rearrange("p a (c d) -> p (a c) d", d=D)
        x1, h1, x1b, y = (late[:, k, :].rearrange("p (t d) -> p t d", t=NT) for k in range(4))
        wv_in, w_in = sb("wv_in", [P, DC, D]), sb("w_in", [P, DC, D])
        unused_a = w_in[:, 0, :].rearrange("p (t n) -> p t n", t=NT)
        unused_h = w_in[:, 1:1 + NT, :]

        st_x, st_1 = sb("st_x", [P, NT, 6]), sb("st_1", [P, NT, 6])
        mv_x, mv_1 = sb("mv_x", [P, NT, 2]), sb("mv_1", [P, NT, 2])
        ve_x, ve_1 = sb("ve_x", [P, NT]), sb("ve_1", [P, NT])
        rs_x, rs_1 = sb("rs_x", [P, NT]), sb("rs_1", [P, NT])
        sc_1 = sb("sc_1", [P, NT])
        nb_x, nb_1 = sb("nb_x", [P, NT]), sb("nb_1", [P, NT])
        vk = sb("vk", [P, NT])
        rsum, rsum1 = sb("rsum", [P, NT]), sb("rsum1", [P, NT])
        dn, d = sb("dn", [P, NT]), sb("d", [P, NT])
        d_pair = sb("d_pair", [P, NT, 2], f32r)
        rinv = sb("rinv", [P, NT])
        s_sum, sd = sb("s_sum", [P, NT]), sb("sd", [P, NT])

        ps = ctx.enter_context(nc.psum_tensor("ps", [P, 8, 512], fp32))
        G, Z, HT, V, O1, AT, SV, R, O = 0, 2, 2, 4, 4, 6, 7, 2, 6

        consts_ready, ident_ready = sem("consts_ready"), sem("ident_ready")
        ident_zero = sem("ident_zero")
        wqk_loaded, wv_loaded, w_loaded = sem("wqk_loaded"), sem("wv_loaded"), sem("w_loaded")
        biases_loaded = sem("biases_loaded")
        m_done, wvt_done = sem("m_done"), sem("wvt_done")
        m_hi_ready, m_lo_ready = sem("m_hi_ready"), sem("m_lo_ready")
        wvt_hi_ready, wvt_lo_ready = sem("wvt_hi_ready"), sem("wvt_lo_ready")
        w_hi_ready, w_lo_ready = sem("w_hi_ready"), sem("w_lo_ready")
        bq_wide_ready, rows_done, rows_ready = sem("bq_wide_ready"), sem("rows_done"), sem("rows_ready")

        x_loaded, adj_loaded, stored = sem("x_loaded"), sem("adj_loaded"), sem("stored")
        bn_x_done, mv_x_done, ve_x_done, rs_x_done, ln_x_ready = (
            sem("bn_x_done"), sem("mv_x_done"), sem("ve_x_done"), sem("rs_x_done"), sem("ln_x_ready"))
        bn_1_done, mv_1_done, ve_1_done, rs_1_done, sc_1_done, ln_1_ready = (
            sem("bn_1_done"), sem("mv_1_done"), sem("ve_1_done"), sem("rs_1_done"), sem("sc_1_done"),
            sem("ln_1_ready"))
        h_ready = sems("h_ready")
        rsum_ready, rsum1_ready, dn_ready, d_ready = (
            sem("rsum_ready"), sem("rsum1_ready"), sem("dn_ready"), sem("d_ready"))
        d_hi_ready, d_pair_ready = sem("d_hi_ready"), sem("d_pair_ready")
        at_done, adjt_ready = sem("at_done"), sem("adjt_ready")
        ht_done, ht_hi_ready, ht_lo_ready = sems("ht_done"), sems("ht_hi_ready"), sems("ht_lo_ready")
        vk_ready = sems("vk_ready")
        g_done, g_hi_ready, g_lo_ready = sems("g_done"), sems("g_hi_ready"), sems("g_lo_ready")
        v_done, v_hi_ready, v_lo_ready = sems("v_done"), sems("v_hi_ready"), sems("v_lo_ready")
        s_done, e_ready, p_ready = sems("s_done"), sems("e_ready"), sems("p_ready")
        p_hi_ready, p_lo_ready = sems("p_hi_ready"), sems("p_lo_ready")
        r_done, rinv_ready, o_done = sem("r_done"), sem("rinv_ready"), sems("o_done")
        xb_ready, x1_ready = sem("xb_ready"), sems("x1_ready")
        hat_hi_ready, hat_ready, hat_lo_ready = sem("hat_hi_ready"), sem("hat_ready"), sem("hat_lo_ready")
        h1_ready, h1_lo_ready = sems("h1_ready"), sems("h1_lo_ready")
        z_done, z_hi_ready, z_lo_ready = sems("z_done"), sems("z_hi_ready"), sems("z_lo_ready")
        sv_done, s_sum_ready, sd_ready, x1b_ready = (
            sem("sv_done"), sem("s_sum_ready"), sem("sd_ready"), sems("x1b_ready"))
        o1_done, y_ready = sems("o1_done"), sems("y_ready")

        block = ctx.enter_context(nc.Block())

        def steps(eng, step):
            step(0, prev=False, main=False, ahead=True)
            step(1, prev=False, main=True, ahead=True)
            step(2, prev=True, main=True, ahead=True, older=False)
            with eng.Fori(3, B) as this:
                step(this, prev=True, main=True, ahead=True)
            step(B, prev=True, main=True, ahead=False)
            step(B + 1, prev=True, main=False, ahead=False)


        @block.sync
        def _(sp):
            sp.dma_start(x_in[:], x[0].rearrange("(t p) d -> p t d", p=P)).then_inc(x_loaded, 16)
            sp.dma_start(adj_in[:], adj[0].rearrange("(t p) n -> p t n", p=P)).then_inc(adj_loaded, 16)
            sp.dma_start(wv_in[:], wv.rearrange("(c p) d -> p c d", p=P)).then_inc(wv_loaded, 16)
            sp.dma_start(w_in[:], w.rearrange("(c p) d -> p c d", p=P)).then_inc(w_loaded, 16)

            adj_flat, x_flat = adj.rearrange("g n m -> (g n m)"), x.rearrange("g n d -> (g n d)")

            def step(this, prev, main, ahead, older=True):
                if main and ahead:
                    adj_next = adj_flat[bass.ds(sp.snap(this * (N * N)), N * N)]
                    x_next = x_flat[bass.ds(sp.snap(this * (N * D)), N * D)]
                    sp.wait_ge(at_done, this)
                    sp.wait_ge(rsum_ready, this)
                    sp.dma_start(adj_in[:], adj_next.rearrange("(t p n) -> p t n", p=P, n=N)).then_inc(adj_loaded, 16)
                    sp.wait_ge(h_ready[1], this)
                    sp.wait_ge(xb_ready, this)
                    sp.dma_start(x_in[:], x_next.rearrange("(t p d) -> p t d", p=P, d=D)).then_inc(x_loaded, 16)
                if prev:
                    for t in range(NT):
                        sp.wait_ge(y_ready[t], this - 1)
                        sp.dma_start(out[this - 2, t * P:(t + 1) * P, :], y[:, t, :]).then_inc(stored, 16)

            steps(sp, step)
            sp.wait_ge(stored, B * 16 * NT)

        @block.gpsimd
        def _(pool):
            pool.memset(ident[:], 0.0)
            pool.memset(eye[:], 0.0).then_inc(ident_zero, 1)
            pool.wait_ge(ident_zero, 1)
            pool.affine_select(out=ident[:], in_=ident[:], compare_op=ALU.not_equal, fill=1.0,
                               base=0, pattern=[[-1, P]], channel_multiplier=1).then_inc(ident_ready, 1)
            pool.affine_select(out=eye[:], in_=eye[:], compare_op=ALU.not_equal, fill=1.0, base=0,
                               pattern=[[P, NT], [-1, N]], channel_multiplier=1)
            pool.memset(minus_half[:], -0.5).then_inc(ident_ready, 1)
            pool.wait_ge(consts_ready, 1)
            pool.wait_ge(ident_ready, 2)

            def step(this, prev, main, ahead, older=True):
                if prev:
                    pool.wait_ge(ve_1_done, this - 1)
                    pool.tensor_tensor(rs_1[:], ve_1[:], minus_half[:], ALU.pow).then_inc(rs_1_done, 1)
                if main:
                    if prev:
                        pool.wait_ge(d_pair_ready, this - 1)
                    pool.wait_ge(rsum_ready, this)
                    pool.tensor_tensor(rsum1[:], rsum[:], ones[:, 0:NT], ALU.add).then_inc(rsum1_ready, 1)
                    pool.wait_ge(rsum1_ready, this)
                    pool.tensor_tensor(dn[:], rsum1[:], minus_half[:], ALU.pow).then_inc(dn_ready, 1)
                    if prev:
                        pool.wait_ge(x1_ready[1], this - 1)
                    else:
                        pool.wait_ge(rows_ready, 1)
                    pool.wait_ge(x_loaded, this * 16)
                    for t in range(NT):
                        last = pool.tensor_tensor(xb[:, t, :], x_in[:, t, :], bv_row[:], ALU.add)
                    last.then_inc(xb_ready, 1)
                if ahead:
                    pool.wait_ge(ve_x_done, this + 1)
                    pool.tensor_tensor(rs_x[:], ve_x[:], minus_half[:], ALU.pow).then_inc(rs_x_done, 1)
                if main:
                    pool.wait_ge(adjt_ready, this)
                    if prev:
                        pool.wait_ge(sv_done, this - 1)
                    pool.tensor_tensor(hat_hi[:], adjt[:], eye[:], ALU.add).then_inc(hat_hi_ready, 1)
                    pool.tensor_tensor(hat[:], adjt[:], eye[:], ALU.add).then_inc(hat_ready, 1)
                    pool.wait_ge(hat_ready, this)
                    pool.tensor_tensor(hat_lo[:], hat[:], hat_hi[:].bitcast(fp32), ALU.subtract).then_inc(hat_lo_ready, 1)

            steps(pool, step)

        @block.scalar
        def _(act):
            act.dma_start(wk_in, wk.rearrange("(c p) d -> p c d", p=P)).then_inc(wqk_loaded, 16)
            act.dma_start(wq_in, wq.rearrange("(c p) d -> p c d", p=P)).then_inc(wqk_loaded, 16)
            act.dma_start(bv_in[:], bv.rearrange("(a n) -> a n", a=1)).then_inc(biases_loaded, 16)
            act.dma_start(b_in[:], b.rearrange("(a n) -> a n", a=1)).then_inc(biases_loaded, 16)
            act.dma_start(bq_col[:], bq.rearrange("(c p) -> p c", p=P), allow_slow_non_contiguous=True).then_inc(biases_loaded, 16)
            act.dma_start(bk_col[:], bk.rearrange("(c p) -> p c", p=P), allow_slow_non_contiguous=True).then_inc(biases_loaded, 16)

            def split_weights():
                for c in range(DC):
                    act.wait_ge(wvt_done, c + 1)
                    act.activation(wvt_hi[:, c, :], ps[:, 4 + c, :], ACT.Copy).then_inc(wvt_hi_ready, 1)
                for c in range(DC):
                    act.wait_ge(m_done, c + 1)
                    act.activation(m_hi[:, c, :], ps[:, c, :], ACT.Copy).then_inc(m_hi_ready, 1)
                act.wait_ge(w_loaded, 16)
                act.activation(w_hi[:], w_in[:], ACT.Copy).then_inc(w_hi_ready, 1)

            def step(this, prev, main, ahead, older=True):
                if prev:
                    act.wait_ge(ln_1_ready, this - 1)
                    for t in range(NT):
                        act.activation(h1[:, t, :], x1[:, t, :], ACT.Relu, scale=sc_1[:, t:t + 1],
                                       bias=nb_1[:, t:t + 1])
                        act.activation(h1_hi[:, t, :], x1[:, t, :], ACT.Relu, scale=sc_1[:, t:t + 1],
                                       bias=nb_1[:, t:t + 1]).then_inc(h1_ready[t], 1)
                if main:
                    for j in range(2):
                        act.wait_ge(g_done[j], this)
                        for m in range(2 * j, 2 * j + 2):
                            last = act.activation(g_hi[:, m, :], ps[:, G + j, m % 2 * N:m % 2 * N + N],
                                                  ACT.Identity, bias=u_col[:, m:m + 1])
                        last.then_inc(g_hi_ready[j], 1)
                if prev:
                    for j in range(2):
                        act.wait_ge(z_done[j], this - 1)
                        act.activation(z_hi[:, 2 * j:2 * j + 2, :].rearrange("p c n -> p (c n)"),
                                       ps[:, Z + j, :], ACT.Copy).then_inc(z_hi_ready[j], 1)
                if ahead:
                    act.wait_ge(ln_x_ready, this + 1)
                    for t in range(NT):
                        act.activation(h[:, t, :], x_in[:, t, :], ACT.Relu, scale=rs_x[:, t:t + 1],
                                       bias=nb_x[:, t:t + 1]).then_inc(h_ready[t], 1)
                    act.wait_ge(adj_loaded, (this + 1) * 16)
                    if main:
                        act.wait_ge(dn_ready, this)
                    else:
                        split_weights()
                        act.wait_ge(w_lo_ready, 1)
                    for t in range(NT):
                        last = act.activation(unused_a[:, t, :], adj_in[:, t, :], ACT.Copy,
                                              accum_out=rsum[:, t:t + 1])
                    last.then_inc(rsum_ready, 1)
                if main:
                    for t in range(NT):
                        act.wait_ge(v_done[t], this)
                        act.activation(v_hi[:, t, :], ps[:, V + t, :], ACT.Copy).then_inc(v_hi_ready[t], 1)
                    for t in range(NT):
                        act.wait_ge(s_done[t], this)
                        act.wait_ge(vk_ready[t], this)
                        act.activation(e[:, t, :], ps[:, G + t, 0:N], ACT.Exp,
                                       bias=vk[:, t:t + 1]).then_inc(e_ready[t], 1)
                    for t in range(NT):
                        act.wait_ge(p_ready[t], this)
                        act.activation(p_hi[:, t, :], p[:, t, :], ACT.Copy).then_inc(p_hi_ready[t], 1)
                if ahead:
                    act.wait_ge(at_done, this + 1)
                    if main:
                        act.wait_ge(hat_ready, this)
                    act.activation(adjt[:].rearrange("p t n -> p (t n)"), ps[:, AT, :],
                                   ACT.Copy).then_inc(adjt_ready, 1)
                    for j in range(2):
                        act.wait_ge(ht_done[j], this + 1)
                        act.activation(ht_hi[:, 2 * j:2 * j + 2, :].rearrange("p c n -> p (c n)"),
                                       ps[:, HT + j, :], ACT.Copy).then_inc(ht_hi_ready[j], 1)

            steps(act, step)

        @block.vector
        def _(dve):
            dve.memset(ones[:], 1.0).then_inc(consts_ready, 1)
            dve.wait_ge(consts_ready, 1)
            dve.tensor_copy(ones_r[:], ones[:, 0:2]).then_inc(consts_ready, 1)
            dve.wait_ge(biases_loaded, 64)
            for c in range(DC):
                last = dve.tensor_scalar(bq_wide[:, c, :], ones[:], bq_col[:, c:c + 1], None, ALU.mult)
            last.then_inc(bq_wide_ready, 1)

            def split_weights():
                for c in range(DC):
                    dve.wait_ge(wvt_hi_ready, c + 1)
                    dve.tensor_tensor(wvt_lo[:, c, :], ps[:, 4 + c, :], wvt_hi[:, c, :].bitcast(fp32),
                                      ALU.subtract).then_inc(wvt_lo_ready, 1)
                for c in range(DC):
                    dve.wait_ge(m_hi_ready, c + 1)
                    dve.tensor_tensor(m_lo[:, c, :], ps[:, c, :], m_hi[:, c, :].bitcast(fp32),
                                      ALU.subtract).then_inc(m_lo_ready, 1)
                dve.wait_ge(w_hi_ready, 1)
                dve.tensor_tensor(w_lo[:], w_in[:], w_hi[:].bitcast(fp32), ALU.subtract).then_inc(w_lo_ready, 1)
                dve.wait_ge(rows_done, 1)
                dve.tensor_copy(bv_row[:], ps[:, 4, :])
                dve.tensor_copy(b_row[:], ps[:, 5, :])
                dve.tensor_copy(c_row[:], ps[:, 6, :])
                dve.tensor_copy(u_col[:], ps[:, 7, 0:DC])
                dve.tensor_copy(bb_col[:], ps[:, 7, DC:DC + 1]).then_inc(rows_ready, 1)
                dve.wait_ge(rows_ready, 1)

            def add_bias(t):
                dve.scalar_tensor_tensor(x1b[:, t, :], b_row[:], sd[:, t:t + 1], x1[:, t, :],
                                         ALU.mult, ALU.add).then_inc(x1b_ready[t], 1)

            def step(this, prev, main, ahead, older=True):
                if prev:
                    if older:
                        dve.wait_ge(y_ready[1], this - 2)
                    dve.wait_ge(dn_ready, this - 1)
                    dve.tensor_copy(d[:], dn[:]).then_inc(d_ready, 1)
                    dve.tensor_copy(d_pair[:, :, 0], dn[:]).then_inc(d_hi_ready, 1)
                    dve.wait_ge(xb_ready, this - 1)
                    dve.wait_ge(rinv_ready, this - 1)
                    for t in range(NT):
                        dve.wait_ge(o_done[t], this - 1)
                        dve.scalar_tensor_tensor(x1[:, t, :], ps[:, O + t, :], rinv[:, t:t + 1], xb[:, t, :],
                                                 ALU.mult, ALU.add).then_inc(x1_ready[t], 1)
                    for t in range(NT):
                        dve.wait_ge(x1_ready[t], this - 1)
                        last = dve.bn_stats(st_1[:, t, :], x1[:, t, :])
                    last.then_inc(bn_1_done, 1)
                    dve.wait_ge(d_hi_ready, this - 1)
                    dve.wait_ge(bn_1_done, this - 1)
                    dve.tensor_tensor(d_pair[:, :, 1], dn[:], d_pair[:, :, 0].bitcast(fp32),
                                      ALU.subtract).then_inc(d_pair_ready, 1)
                    for t in range(NT):
                        last = dve.bn_aggr(mv_1[:, t, :], st_1[:, t, :])
                    last.then_inc(mv_1_done, 1)
                    dve.wait_ge(mv_1_done, this - 1)
                    dve.tensor_scalar(ve_1[:], mv_1[:, :, 1], EPS, None, ALU.add).then_inc(ve_1_done, 1)
                    dve.wait_ge(rs_1_done, this - 1)
                    dve.tensor_tensor(sc_1[:], rs_1[:], d[:], ALU.mult).then_inc(sc_1_done, 1)
                    dve.wait_ge(sc_1_done, this - 1)
                    dve.scalar_tensor_tensor(nb_1[:], mv_1[:, :, 0], -1.0, sc_1[:], ALU.mult,
                                             ALU.mult).then_inc(ln_1_ready, 1)
                    for t in range(NT):
                        dve.wait_ge(h1_ready[t], this - 1)
                        dve.tensor_tensor(h1_lo[:, t, :], h1[:, t, :], h1_hi[:, t, :].bitcast(fp32),
                                          ALU.subtract).then_inc(h1_lo_ready[t], 1)
                if main:
                    for j in range(2):
                        dve.wait_ge(g_hi_ready[j], this)
                        for m in range(2 * j, 2 * j + 2):
                            last = dve.scalar_tensor_tensor(
                                g_lo[:, m, :], ps[:, G + j, m % 2 * N:m % 2 * N + N], u_col[:, m:m + 1],
                                g_hi[:, m, :].bitcast(fp32), ALU.add, ALU.subtract)
                        last.then_inc(g_lo_ready[j], 1)
                if prev:
                    for j in range(2):
                        dve.wait_ge(z_hi_ready[j], this - 1)
                        dve.tensor_tensor(z_lo[:, 2 * j:2 * j + 2, :].rearrange("p c n -> p (c n)"),
                                          ps[:, Z + j, :],
                                          z_hi[:, 2 * j:2 * j + 2, :].rearrange("p c n -> p (c n)").bitcast(fp32),
                                          ALU.subtract).then_inc(z_lo_ready[j], 1)
                    dve.wait_ge(sv_done, this - 1)
                    dve.tensor_reduce(s_sum[:], ps[:, SV, 0:2 * NT].rearrange("p (t a) -> p t a", a=2),
                                      axis=AX.X, op=ALU.add).then_inc(s_sum_ready, 1)
                    dve.wait_ge(s_sum_ready, this - 1)
                    dve.tensor_tensor(sd[:], s_sum[:], d[:], ALU.mult).then_inc(sd_ready, 1)
                    dve.wait_ge(sd_ready, this - 1)
                    add_bias(0)
                    if not ahead:
                        add_bias(1)
                if ahead:
                    dve.wait_ge(x_loaded, (this + 1) * 16)
                    for t in range(NT):
                        last = dve.bn_stats(st_x[:, t, :], x_in[:, t, :])
                    last.then_inc(bn_x_done, 1)
                    dve.wait_ge(bn_x_done, this + 1)
                    if prev:
                        add_bias(1)
                    for t in range(NT):
                        last = dve.bn_aggr(mv_x[:, t, :], st_x[:, t, :])
                    last.then_inc(mv_x_done, 1)
                    dve.wait_ge(mv_x_done, this + 1)
                    dve.tensor_scalar(ve_x[:], mv_x[:, :, 1], EPS, None, ALU.add).then_inc(ve_x_done, 1)
                    dve.wait_ge(rs_x_done, this + 1)
                    dve.scalar_tensor_tensor(nb_x[:], mv_x[:, :, 0], -1.0, rs_x[:], ALU.mult,
                                             ALU.mult).then_inc(ln_x_ready, 1)
                    if not main:
                        split_weights()
                if main:
                    for t in range(NT):
                        dve.wait_ge(v_hi_ready[t], this)
                        dve.tensor_tensor(v_lo[:, t, :], ps[:, V + t, :], v_hi[:, t, :].bitcast(fp32),
                                          ALU.subtract).then_inc(v_lo_ready[t], 1)
                    dve.wait_ge(adjt_ready, this)
                    for t in range(NT):
                        dve.wait_ge(e_ready[t], this)
                        dve.tensor_tensor(p[:, t, :], e[:, t, :], adjt[:, t, :], ALU.mult).then_inc(p_ready[t], 1)
                if ahead:
                    for t in range(NT):
                        dve.wait_ge(h_ready[t], this + 1)
                        dve.tensor_tensor_reduce(out=unused_h[:, t, :], in0=h[:, t, :], in1=c_row[:], scale=1.0,
                                                 scalar=bb_col[:, 0:1], op0=ALU.mult, op1=ALU.add,
                                                 accum_out=vk[:, t:t + 1]).then_inc(vk_ready[t], 1)
                if main:
                    for t in range(NT):
                        dve.wait_ge(p_hi_ready[t], this)
                        dve.tensor_tensor(p_lo[:, t, :], p[:, t, :], p_hi[:, t, :].bitcast(fp32),
                                          ALU.subtract).then_inc(p_lo_ready[t], 1)
                if ahead:
                    for j in range(2):
                        dve.wait_ge(ht_hi_ready[j], this + 1)
                        dve.tensor_tensor(ht_lo[:, 2 * j:2 * j + 2, :].rearrange("p c n -> p (c n)"),
                                          ps[:, HT + j, :],
                                          ht_hi[:, 2 * j:2 * j + 2, :].rearrange("p c n -> p (c n)").bitcast(fp32),
                                          ALU.subtract).then_inc(ht_lo_ready[j], 1)
                if prev:
                    if older:
                        dve.wait_ge(stored, (this - 2) * (16 * NT))
                    for t in range(NT):
                        dve.wait_ge(o1_done[t], this - 1)
                        dve.wait_ge(x1b_ready[t], this - 1)
                        dve.scalar_tensor_tensor(y[:, t, :], ps[:, O1 + t, :], d[:, t:t + 1], x1b[:, t, :],
                                                 ALU.mult, ALU.add).then_inc(y_ready[t], 1)
                if main:
                    dve.wait_ge(r_done, this)
                    dve.reciprocal(rinv[:], ps[:, R, 0:2 * NT:2]).then_inc(rinv_ready, 1)

            steps(dve, step)

        @block.tensor
        def _(pe):
            def product(dst, pairs, cols):
                n = 0
                for stationary, moving in pairs:
                    for c in range(cols):
                        last = pe.matmul(dst, stationary(c), moving(c), start=(n == 0),
                                         stop=(n == len(pairs) * cols - 1))
                        n += 1
                return last

            def weights():
                pe.wait_ge(wv_loaded, 16)
                for c in range(DC):
                    for o in range(DC):
                        last = pe.transpose(ps[:, 4 + c, o * P:(o + 1) * P], wv_in[:, o, c * P:(c + 1) * P], ident[:])
                    last.then_inc(wvt_done, 1)
                pe.wait_ge(wqk_loaded, 32)
                for c in range(DC):
                    product(ps[:, c, :], [(lambda o, c=c: wk_in[:, o, c * P:(c + 1) * P], lambda o: wq_in[:, o, :])],
                            DC).then_inc(m_done, 1)
                pe.wait_ge(biases_loaded, 64)
                pe.wait_ge(consts_ready, 1)
                pe.wait_ge(bq_wide_ready, 1)
                pe.wait_ge(wvt_lo_ready, DC)
                pe.matmul(ps[:, 4, :], ones[0:1, :], bv_in[:], start=True, stop=True)
                pe.matmul(ps[:, 5, :], ones[0:1, :], b_in[:], start=True, stop=True)
                product(ps[:, 6, :], [(lambda o: bq_wide[:, o, :], lambda o: wk_in[:, o, :])], DC)
                for m in range(DC):
                    product(ps[:, 7, m:m + 1], [(lambda o, m=m: wq_in[:, o, m * P:(m + 1) * P],
                                                 lambda o: bk_col[:, o:o + 1])], DC)
                product(ps[:, 7, DC:DC + 1], [(lambda o: bq_wide[:, o, :], lambda o: bk_col[:, o:o + 1])],
                        DC).then_inc(rows_done, 1)
                pe.wait_ge(rows_ready, 1)
                pe.wait_ge(m_lo_ready, DC)

            def step(this, prev, main, ahead, older=True):
                if main:
                    pe.wait_ge(ht_lo_ready[0], this)
                    pe.wait_ge(ht_lo_ready[1], this)
                    for m in range(DC):
                        cols = slice(m * P, (m + 1) * P)
                        last = product(ps[:, G + m // 2, m % 2 * N:m % 2 * N + N],
                                       [(lambda c: m_hi[:, c, cols], lambda c: ht_hi[:, c, :]),
                                        (lambda c: m_hi[:, c, cols], lambda c: ht_lo[:, c, :]),
                                        (lambda c: m_lo[:, c, cols], lambda c: ht_hi[:, c, :])], DC)
                        if m % 2:
                            last.then_inc(g_done[m // 2], 1)
                if prev:
                    pe.wait_ge(hat_lo_ready, this - 1)
                    pe.wait_ge(h1_lo_ready[0], this - 1)
                    pe.wait_ge(h1_lo_ready[1], this - 1)
                    for m in range(DC):
                        cols = slice(m * P, (m + 1) * P)
                        last = product(ps[:, Z + m // 2, m % 2 * N:m % 2 * N + N],
                                       [(lambda c: h1_hi[:, c, cols], lambda c: hat_hi[:, c, :]),
                                        (lambda c: h1_hi[:, c, cols], lambda c: hat_lo[:, c, :]),
                                        (lambda c: h1_lo[:, c, cols], lambda c: hat_hi[:, c, :])], NT)
                        if m % 2:
                            last.then_inc(z_done[m // 2], 1)
                    pe.wait_ge(d_pair_ready, this - 1)
                    for t in range(NT):
                        cols = slice(t * P, (t + 1) * P)
                        last = product(ps[:, SV, 2 * t:2 * t + 2],
                                       [(lambda c: hat_hi[:, c, cols], lambda c: d_pair[:, c, :]),
                                        (lambda c: hat_lo[:, c, cols], lambda c: d_pair[:, c, :])], NT)
                    last.then_inc(sv_done, 1)
                if main:
                    for t in range(NT):
                        cols = slice(t * P, (t + 1) * P)
                        product(ps[:, V + t, :],
                                [(lambda c: ht_hi[:, c, cols], lambda c: wvt_hi[:, c, :]),
                                 (lambda c: ht_hi[:, c, cols], lambda c: wvt_lo[:, c, :]),
                                 (lambda c: ht_lo[:, c, cols], lambda c: wvt_hi[:, c, :])],
                                DC).then_inc(v_done[t], 1)
                    pe.wait_ge(g_lo_ready[0], this)
                    pe.wait_ge(g_lo_ready[1], this)
                    for t in range(NT):
                        cols = slice(t * P, (t + 1) * P)
                        product(ps[:, G + t, 0:N],
                                [(lambda c: g_hi[:, c, cols], lambda c: ht_hi[:, c, :]),
                                 (lambda c: g_hi[:, c, cols], lambda c: ht_lo[:, c, :]),
                                 (lambda c: g_lo[:, c, cols], lambda c: ht_hi[:, c, :])],
                                DC).then_inc(s_done[t], 1)
                if ahead:
                    if not main:
                        pe.wait_ge(ident_ready, 1)
                        weights()
                    pe.wait_ge(adj_loaded, (this + 1) * 16)
                    for k in range(NT):
                        for q in range(NT):
                            last = pe.transpose(ps[:, AT, k * N + q * P:k * N + (q + 1) * P],
                                                adj_in[:, q, k * P:(k + 1) * P], ident[:])
                    last.then_inc(at_done, 1)
                    pe.wait_ge(h_ready[0], this + 1)
                    pe.wait_ge(h_ready[1], this + 1)
                    if prev:
                        pe.wait_ge(z_lo_ready[0], this - 1)
                        pe.wait_ge(z_lo_ready[1], this - 1)
                    for c in range(DC):
                        for t in range(NT):
                            last = pe.transpose(ps[:, HT + c // 2, c % 2 * N + t * P:c % 2 * N + (t + 1) * P],
                                                h[:, t, c * P:(c + 1) * P], ident[:])
                        if c % 2:
                            last.then_inc(ht_done[c // 2], 1)
                if prev:
                    pe.wait_ge(w_lo_ready, 1)
                    pe.wait_ge(z_lo_ready[0], this - 1)
                    pe.wait_ge(z_lo_ready[1], this - 1)
                    for t in range(NT):
                        if main:
                            pe.wait_ge(v_lo_ready[t], this)
                        cols = slice(t * P, (t + 1) * P)
                        product(ps[:, O1 + t, :],
                                [(lambda c: z_hi[:, c, cols], lambda c: w_hi[:, c, :]),
                                 (lambda c: z_hi[:, c, cols], lambda c: w_lo[:, c, :]),
                                 (lambda c: z_lo[:, c, cols], lambda c: w_hi[:, c, :])],
                                DC).then_inc(o1_done[t], 1)
                if main:
                    pe.wait_ge(p_lo_ready[0], this)
                    pe.wait_ge(p_lo_ready[1], this)
                    pe.wait_ge(consts_ready, 2)
                    if ahead:
                        pe.wait_ge(ht_lo_ready[0], this + 1)
                    for t in range(NT):
                        cols = slice(t * P, (t + 1) * P)
                        last = product(ps[:, R, 2 * t:2 * t + 2],
                                       [(lambda c: p_hi[:, c, cols], lambda c: ones_r[:]),
                                        (lambda c: p_lo[:, c, cols], lambda c: ones_r[:])], NT)
                    last.then_inc(r_done, 1)
                    pe.wait_ge(v_lo_ready[0], this)
                    pe.wait_ge(v_lo_ready[1], this)
                    if ahead:
                        pe.wait_ge(adjt_ready, this + 1)
                    if prev:
                        pe.wait_ge(s_sum_ready, this - 1)
                    for t in range(NT):
                        cols = slice(t * P, (t + 1) * P)
                        product(ps[:, O + t, :],
                                [(lambda c: p_hi[:, c, cols], lambda c: v_hi[:, c, :]),
                                 (lambda c: p_hi[:, c, cols], lambda c: v_lo[:, c, :]),
                                 (lambda c: p_lo[:, c, cols], lambda c: v_hi[:, c, :])],
                                NT).then_inc(o_done[t], 1)

            steps(pe, step)


_INS = ["x", "adj", "L0_gnn_Wq_w", "L0_gnn_Wq_b", "L0_gnn_Wk_w", "L0_gnn_Wk_b", "L0_gnn_Wv_w", "L0_gnn_Wv_b",
        "L1_gnn_W", "L1_gnn_b"]


def kernel(**inputs):
    import numpy as _np
    import concourse.bacc as _bacc
    from concourse import mybir as _mybir
    from concourse.bass_utils import run_bass_kernel_spmd as _run

    nc = _bacc.Bacc("TRN2", target_bir_lowering=False, num_devices=1)
    arrays, args = {}, []
    for name in _INS:
        a = _np.ascontiguousarray(inputs[name])
        arrays[f"in_{name}_dram"] = a
        args.append(nc.dram_tensor(f"in_{name}_dram", a.shape, _mybir.dt.from_np(a.dtype), kind="ExternalInput").ap())
    out = nc.dram_tensor("out_dram", (B, N, D), _mybir.dt.float32, kind="ExternalOutput").ap()
    gnn_program(nc, *args, out)
    r = _run(nc, [arrays], core_ids=[0])
    return r.results[0]["out_dram"]
```

```python
import concourse.bass as bass
from concourse import mybir
from contextlib import ExitStack

B, N, D = 64, 256, 512
P = 128
NT = N // P
DC = D // P
HD = D // 2
EPS = 1e-5


def gnn_program(nc, x, adj, wq, bq, wk, bk, wv, bv, w, b, out):
    fp32, f32r = mybir.dt.float32, mybir.dt.float32r
    ALU, ACT, AX = mybir.AluOpType, mybir.ActivationFunctionType, mybir.AxisListType

    ctx = ExitStack()
    with ctx:
        def sb(name, shape, dt=fp32):
            return ctx.enter_context(nc.sbuf_tensor(name, shape, dt))

        def sem(name):
            return ctx.enter_context(nc.semaphore(name))

        def sems(name, n=2):
            return [sem(f"{name}{k}") for k in range(n)]

        m_hi, m_lo = sb("m_hi", [P, DC, D], f32r), sb("m_lo", [P, DC, D], f32r)
        wvt_hi, wvt_lo = sb("wvt_hi", [P, DC, D], f32r), sb("wvt_lo", [P, DC, D], f32r)
        w_hi, w_lo = sb("w_hi", [P, DC, D], f32r), sb("w_lo", [P, DC, D], f32r)
        u_col = sb("u_col", [P, DC])
        c_row = sb("c_row", [P, D])
        bb_col = sb("bb_col", [P, 1])
        bv_row, b_row = sb("bv_row", [P, D]), sb("b_row", [P, D])
        ident = sb("ident", [P, P])
        eye = sb("eye", [P, NT, N])
        ones = sb("ones", [P, P])
        minus_half = sb("minus_half", [P, NT])
        bq_col, bk_col = sb("bq_col", [P, DC]), sb("bk_col", [P, DC])
        bq_wide = sb("bq_wide", [P, DC, P])
        bv_in, b_in = sb("bv_in", [1, D]), sb("b_in", [1, D])

        x_in = sb("x_in", [P, NT, D])
        adj_in = sb("adj_in", [P, NT, N])
        h = sb("h", [P, NT, D])
        ht_hi, ht_lo = sb("ht_hi", [P, DC, N], f32r), sb("ht_lo", [P, DC, N], f32r)
        g_hi, g_lo = sb("g_hi", [P, DC, N], f32r), sb("g_lo", [P, DC, N], f32r)
        adjt = sb("adjt", [P, NT, N])
        e = sb("e", [P, NT, N])
        p = sb("p", [P, NT, N])
        p_hi, p_lo = sb("p_hi", [P, NT, N], f32r), sb("p_lo", [P, NT, N], f32r)
        v_hi, v_lo = sb("v_hi", [P, NT, 2, HD + 2], f32r), sb("v_lo", [P, NT, 2, HD + 2], f32r)
        xb = sb("xb", [P, NT, D])
        hat = sb("hat", [P, NT, N])
        hat_hi, hat_lo = sb("hat_hi", [P, NT, N], f32r), sb("hat_lo", [P, NT, N], f32r)
        h1_hi, h1_lo = sb("h1_hi", [P, NT, D], f32r), sb("h1_lo", [P, NT, D], f32r)
        z_hi, z_lo = sb("z_hi", [P, DC, N], f32r), sb("z_lo", [P, DC, N], f32r)
        late = sb("late", [P, 4, NT * D])
        wq_in = late[:, 0:2, :].rearrange("p a (c d) -> p (a c) d", d=D)
        wk_in = late[:, 2:4, :].rearrange("p a (c d) -> p (a c) d", d=D)
        x1, h1, x1b, y = (late[:, k, :].rearrange("p (t d) -> p t d", t=NT) for k in range(4))
        wv_in, w_in = sb("wv_in", [P, DC, D]), sb("w_in", [P, DC, D])
        adj_kept = w_in[:, 0, :].rearrange("p (t n) -> p t n", t=NT)
        unused_h = w_in[:, 1:1 + NT, :]
        unused_a = w_in[:, 3, :].rearrange("p (t n) -> p t n", t=NT)

        st_x, st_1 = sb("st_x", [P, NT, 6]), sb("st_1", [P, NT, 6])
        mv_x, mv_1 = sb("mv_x", [P, NT, 2]), sb("mv_1", [P, NT, 2])
        ve_x, ve_1 = sb("ve_x", [P, NT]), sb("ve_1", [P, NT])
        rs_x, rs_1 = sb("rs_x", [P, NT]), sb("rs_1", [P, NT])
        sc_1 = sb("sc_1", [P, NT])
        nb_x, nb_1 = sb("nb_x", [P, NT]), sb("nb_1", [P, NT])
        vk = sb("vk", [P, NT])
        rsum, rsum1 = sb("rsum", [P, NT]), sb("rsum1", [P, NT])
        dn, d = sb("dn", [P, NT]), sb("d", [P, NT])
        rinv = sb("rinv", [P, NT])
        s_sum, sd = sb("s_sum", [P, NT]), sb("sd", [P, NT])

        ps = ctx.enter_context(nc.psum_tensor("ps", [P, 8, 512], fp32))
        G, Z, HT, V, O1, AT, DR = 0, 2, 2, 4, 4, 6, 7
        O = (6, 2)

        consts_ready, ident_ready = sem("consts_ready"), sem("ident_ready")
        ident_zero = sem("ident_zero")
        wqk_loaded, wv_loaded, w_loaded = sem("wqk_loaded"), sem("wv_loaded"), sem("w_loaded")
        biases_loaded = sem("biases_loaded")
        m_done, wvt_done = sem("m_done"), sem("wvt_done")
        m_hi_ready, m_lo_ready = sem("m_hi_ready"), sem("m_lo_ready")
        wvt_hi_ready, wvt_lo_ready = sem("wvt_hi_ready"), sem("wvt_lo_ready")
        w_hi_ready, w_lo_ready = sem("w_hi_ready"), sem("w_lo_ready")
        bq_wide_ready, rows_done, rows_ready = sem("bq_wide_ready"), sem("rows_done"), sem("rows_ready")

        x_loaded, adj_loaded, stored = sem("x_loaded"), sem("adj_loaded"), sem("stored")
        bn_x_done, mv_x_done, ve_x_done, rs_x_done, ln_x_ready = (
            sem("bn_x_done"), sem("mv_x_done"), sem("ve_x_done"), sem("rs_x_done"), sem("ln_x_ready"))
        bn_1_done, mv_1_done, ve_1_done, rs_1_done, sc_1_done, ln_1_ready = (
            sem("bn_1_done"), sem("mv_1_done"), sem("ve_1_done"), sem("rs_1_done"), sem("sc_1_done"),
            sem("ln_1_ready"))
        h_ready = sems("h_ready")
        rsum_ready, rsum1_ready, dn_ready, d_ready = (
            sem("rsum_ready"), sem("rsum1_ready"), sem("dn_ready"), sem("d_ready"))
        at_done, adjt_ready = sem("at_done"), sem("adjt_ready")
        ht_done, ht_hi_ready, ht_lo_ready = sems("ht_done"), sems("ht_hi_ready"), sems("ht_lo_ready")
        vk_ready = sems("vk_ready")
        g_done, g_hi_ready, g_lo_ready = sems("g_done"), sems("g_hi_ready"), sems("g_lo_ready")
        v_done, v_hi_ready, v_lo_ready = sems("v_done"), sems("v_hi_ready"), sems("v_lo_ready")
        s_done, e_ready, p_ready = sems("s_done"), sems("e_ready"), sems("p_ready")
        p_hi_ready, p_lo_ready = sems("p_hi_ready"), sems("p_lo_ready")
        rinv_ready, o_done = sems("rinv_ready"), sems("o_done")
        xb_ready, x1_ready = sem("xb_ready"), sems("x1_ready")
        hat_hi_ready, hat_ready, hat_lo_ready = sem("hat_hi_ready"), sem("hat_ready"), sem("hat_lo_ready")
        h1_ready, h1_lo_ready = sems("h1_ready"), sems("h1_lo_ready")
        z_done, z_hi_ready, z_lo_ready = sems("z_done"), sems("z_hi_ready"), sems("z_lo_ready")
        dr_done, s_sum_ready, sd_ready, x1b_ready = (
            sem("dr_done"), sem("s_sum_ready"), sem("sd_ready"), sems("x1b_ready"))
        o1_done, y_ready = sems("o1_done"), sems("y_ready")

        block = ctx.enter_context(nc.Block())

        def halves(row):
            return row.rearrange("p (a n) -> p a n", a=2)

        def steps(eng, step):
            step(0, prev=False, main=False, ahead=True)
            step(1, prev=False, main=True, ahead=True)
            step(2, prev=True, main=True, ahead=True, older=False)
            with eng.Fori(3, B) as this:
                step(this, prev=True, main=True, ahead=True)
            step(B, prev=True, main=True, ahead=False)
            step(B + 1, prev=True, main=False, ahead=False)


        @block.sync
        def _(sp):
            sp.dma_start(x_in[:], x[0].rearrange("(t p) d -> p t d", p=P)).then_inc(x_loaded, 16)
            sp.dma_start(adj_in[:], adj[0].rearrange("(t p) n -> p t n", p=P)).then_inc(adj_loaded, 16)
            sp.dma_start(wv_in[:], wv.rearrange("(c p) d -> p c d", p=P)).then_inc(wv_loaded, 16)
            sp.dma_start(w_in[:], w.rearrange("(c p) d -> p c d", p=P)).then_inc(w_loaded, 16)

            adj_flat, x_flat = adj.rearrange("g n m -> (g n m)"), x.rearrange("g n d -> (g n d)")

            def step(this, prev, main, ahead, older=True):
                if main and ahead:
                    adj_next = adj_flat[bass.ds(sp.snap(this * (N * N)), N * N)]
                    x_next = x_flat[bass.ds(sp.snap(this * (N * D)), N * D)]
                    sp.wait_ge(at_done, this)
                    sp.wait_ge(rsum_ready, this)
                    sp.dma_start(adj_in[:], adj_next.rearrange("(t p n) -> p t n", p=P, n=N)).then_inc(adj_loaded, 16)
                    sp.wait_ge(h_ready[1], this)
                    sp.wait_ge(xb_ready, this)
                    sp.dma_start(x_in[:], x_next.rearrange("(t p d) -> p t d", p=P, d=D)).then_inc(x_loaded, 16)
                if prev:
                    for t in range(NT):
                        sp.wait_ge(y_ready[t], this - 1)
                        sp.dma_start(out[this - 2, t * P:(t + 1) * P, :], y[:, t, :]).then_inc(stored, 16)

            steps(sp, step)
            sp.wait_ge(stored, B * 16 * NT)

        @block.gpsimd
        def _(pool):
            pool.memset(ident[:], 0.0)
            pool.memset(eye[:], 0.0).then_inc(ident_zero, 1)
            pool.wait_ge(ident_zero, 1)
            pool.affine_select(out=ident[:], in_=ident[:], compare_op=ALU.not_equal, fill=1.0,
                               base=0, pattern=[[-1, P]], channel_multiplier=1).then_inc(ident_ready, 1)
            pool.affine_select(out=eye[:], in_=eye[:], compare_op=ALU.not_equal, fill=1.0, base=0,
                               pattern=[[P, NT], [-1, N]], channel_multiplier=1)
            pool.memset(minus_half[:], -0.5).then_inc(ident_ready, 1)
            pool.wait_ge(consts_ready, 1)
            pool.wait_ge(ident_ready, 2)

            def step(this, prev, main, ahead, older=True):
                if main:
                    if not prev:
                        pool.wait_ge(rows_ready, 1)
                    pool.wait_ge(x_loaded, this * 16)
                    for t in range(NT):
                        if prev:
                            pool.wait_ge(x1_ready[t], this - 1)
                        last = pool.tensor_tensor(xb[:, t, :], x_in[:, t, :], bv_row[:], ALU.add)
                    last.then_inc(xb_ready, 1)
                if prev:
                    pool.wait_ge(ve_1_done, this - 1)
                    pool.tensor_tensor(rs_1[:], ve_1[:], minus_half[:], ALU.pow).then_inc(rs_1_done, 1)
                if main:
                    if prev:
                        pool.wait_ge(d_ready, this - 1)
                    pool.wait_ge(rsum_ready, this)
                    pool.tensor_tensor(rsum1[:], rsum[:], ones[:, 0:NT], ALU.add).then_inc(rsum1_ready, 1)
                    pool.wait_ge(rsum1_ready, this)
                    pool.tensor_tensor(dn[:], rsum1[:], minus_half[:], ALU.pow).then_inc(dn_ready, 1)
                if ahead:
                    pool.wait_ge(ve_x_done, this + 1)
                    pool.tensor_tensor(rs_x[:], ve_x[:], minus_half[:], ALU.pow).then_inc(rs_x_done, 1)
                if main:
                    pool.wait_ge(adjt_ready, this)
                    if prev:
                        pool.wait_ge(z_done[1], this - 1)
                    pool.tensor_tensor(hat_hi[:], adjt[:], eye[:], ALU.add).then_inc(hat_hi_ready, 1)
                    pool.tensor_tensor(hat[:], adjt[:], eye[:], ALU.add).then_inc(hat_ready, 1)
                    pool.wait_ge(hat_ready, this)
                    pool.tensor_tensor(hat_lo[:], hat[:], hat_hi[:].bitcast(fp32), ALU.subtract).then_inc(hat_lo_ready, 1)

            steps(pool, step)

        @block.scalar
        def _(act):
            act.dma_start(wk_in, wk.rearrange("(c p) d -> p c d", p=P)).then_inc(wqk_loaded, 16)
            act.dma_start(wq_in, wq.rearrange("(c p) d -> p c d", p=P)).then_inc(wqk_loaded, 16)
            act.dma_start(bv_in[:], bv.rearrange("(a n) -> a n", a=1)).then_inc(biases_loaded, 16)
            act.dma_start(b_in[:], b.rearrange("(a n) -> a n", a=1)).then_inc(biases_loaded, 16)
            act.dma_start(bq_col[:], bq.rearrange("(c p) -> p c", p=P), allow_slow_non_contiguous=True).then_inc(biases_loaded, 16)
            act.dma_start(bk_col[:], bk.rearrange("(c p) -> p c", p=P), allow_slow_non_contiguous=True).then_inc(biases_loaded, 16)

            def split_weights():
                for c in range(DC):
                    act.wait_ge(wvt_done, c + 1)
                    act.activation(wvt_hi[:, c, :], ps[:, 4 + c, :], ACT.Copy).then_inc(wvt_hi_ready, 1)
                for c in range(DC):
                    act.wait_ge(m_done, c + 1)
                    act.activation(m_hi[:, c, :], ps[:, c, :], ACT.Copy).then_inc(m_hi_ready, 1)
                act.wait_ge(w_loaded, 16)
                act.activation(w_hi[:], w_in[:], ACT.Copy).then_inc(w_hi_ready, 1)

            def value_high(t, this):
                act.wait_ge(v_done[t], this)
                act.activation(v_hi[:, t, :, 0:HD], halves(ps[:, V + t, :]), ACT.Copy).then_inc(v_hi_ready[t], 1)

            def step(this, prev, main, ahead, older=True):
                if prev:
                    act.wait_ge(ln_1_ready, this - 1)
                    for t in range(NT):
                        act.activation(h1[:, t, :], x1[:, t, :], ACT.Relu, scale=sc_1[:, t:t + 1],
                                       bias=nb_1[:, t:t + 1])
                        act.activation(h1_hi[:, t, :], x1[:, t, :], ACT.Relu, scale=sc_1[:, t:t + 1],
                                       bias=nb_1[:, t:t + 1]).then_inc(h1_ready[t], 1)
                if main:
                    for j in range(2):
                        act.wait_ge(g_done[j], this)
                        for m in range(2 * j, 2 * j + 2):
                            last = act.activation(g_hi[:, m, :], ps[:, G + j, m % 2 * N:m % 2 * N + N],
                                                  ACT.Identity, bias=u_col[:, m:m + 1])
                        last.then_inc(g_hi_ready[j], 1)
                if main:
                    value_high(0, this)
                    value_high(1, this)
                if ahead:
                    act.wait_ge(ln_x_ready, this + 1)
                    for t in range(NT):
                        act.activation(h[:, t, :], x_in[:, t, :], ACT.Relu, scale=rs_x[:, t:t + 1],
                                       bias=nb_x[:, t:t + 1]).then_inc(h_ready[t], 1)
                    if not main:
                        split_weights()
                if prev:
                    for j in range(2):
                        act.wait_ge(z_done[j], this - 1)
                        act.activation(z_hi[:, 2 * j:2 * j + 2, :].rearrange("p c n -> p (c n)"),
                                       ps[:, Z + j, :], ACT.Copy).then_inc(z_hi_ready[j], 1)
                if main:
                    for t in range(NT):
                        act.wait_ge(s_done[t], this)
                        act.wait_ge(vk_ready[t], this)
                        act.activation(e[:, t, :], ps[:, G + t, 0:N], ACT.Exp,
                                       bias=vk[:, t:t + 1]).then_inc(e_ready[t], 1)
                    for t in range(NT):
                        act.wait_ge(p_ready[t], this)
                        act.activation(p_hi[:, t, :], p[:, t, :], ACT.Copy).then_inc(p_hi_ready[t], 1)
                if ahead:
                    act.wait_ge(at_done, this + 1)
                    if main:
                        act.wait_ge(hat_ready, this)
                    act.activation(adjt[:].rearrange("p t n -> p (t n)"), ps[:, AT, :],
                                   ACT.Copy).then_inc(adjt_ready, 1)
                    for j in range(2):
                        act.wait_ge(ht_done[j], this + 1)
                        act.activation(ht_hi[:, 2 * j:2 * j + 2, :].rearrange("p c n -> p (c n)"),
                                       ps[:, HT + j, :], ACT.Copy).then_inc(ht_hi_ready[j], 1)
                    act.wait_ge(adj_loaded, (this + 1) * 16)
                    if main:
                        act.wait_ge(sd_ready, this)
                    else:
                        act.wait_ge(w_lo_ready, 1)
                    for t in range(NT):
                        last = act.activation(adj_kept[:, t, :], adj_in[:, t, :], ACT.Copy,
                                              accum_out=rsum[:, t:t + 1])
                    last.then_inc(rsum_ready, 1)

            steps(act, step)

        @block.vector
        def _(dve):
            dve.memset(ones[:], 1.0).then_inc(consts_ready, 1)
            dve.wait_ge(consts_ready, 1)
            dve.tensor_copy(v_hi[:, :, 0, HD:HD + 2], ones[:, 0:2 * NT].rearrange("p (t a) -> p t a", t=NT))
            dve.tensor_scalar(v_lo[:, :, 0, HD:HD + 2], ones[:, 0:2 * NT].rearrange("p (t a) -> p t a", t=NT),
                              0.0, None, ALU.mult).then_inc(consts_ready, 1)
            dve.wait_ge(biases_loaded, 64)
            for c in range(DC):
                last = dve.tensor_scalar(bq_wide[:, c, :], ones[:], bq_col[:, c:c + 1], None, ALU.mult)
            last.then_inc(bq_wide_ready, 1)

            def split_weights():
                for c in range(DC):
                    dve.wait_ge(wvt_hi_ready, c + 1)
                    dve.tensor_tensor(wvt_lo[:, c, :], ps[:, 4 + c, :], wvt_hi[:, c, :].bitcast(fp32),
                                      ALU.subtract).then_inc(wvt_lo_ready, 1)
                for c in range(DC):
                    dve.wait_ge(m_hi_ready, c + 1)
                    dve.tensor_tensor(m_lo[:, c, :], ps[:, c, :], m_hi[:, c, :].bitcast(fp32),
                                      ALU.subtract).then_inc(m_lo_ready, 1)
                dve.wait_ge(w_hi_ready, 1)
                dve.tensor_tensor(w_lo[:], w_in[:], w_hi[:].bitcast(fp32), ALU.subtract).then_inc(w_lo_ready, 1)
                dve.wait_ge(rows_done, 1)
                dve.tensor_copy(bv_row[:], ps[:, 4, :])
                dve.tensor_copy(b_row[:], ps[:, 5, :])
                dve.tensor_copy(c_row[:], ps[:, 6, :])
                dve.tensor_copy(u_col[:], ps[:, 7, 0:DC])
                dve.tensor_copy(bb_col[:], ps[:, 7, DC:DC + 1]).then_inc(rows_ready, 1)
                dve.wait_ge(rows_ready, 1)

            def value_low(t, this):
                dve.wait_ge(v_hi_ready[t], this)
                dve.tensor_tensor(v_lo[:, t, :, 0:HD], halves(ps[:, V + t, :]), v_hi[:, t, :, 0:HD].bitcast(fp32),
                                  ALU.subtract).then_inc(v_lo_ready[t], 1)

            def step(this, prev, main, ahead, older=True):
                if prev:
                    dve.wait_ge(xb_ready, this - 1)
                    for t in range(NT):
                        dve.wait_ge(o_done[t], this - 1)
                        dve.reciprocal(rinv[:, t:t + 1], ps[:, O[t], HD:HD + 1]).then_inc(rinv_ready[t], 1)
                        dve.wait_ge(rinv_ready[t], this - 1)
                        dve.scalar_tensor_tensor(halves(x1[:, t, :]), ps[:, O[t]:O[t] + 2, 0:HD], rinv[:, t:t + 1],
                                                 halves(xb[:, t, :]), ALU.mult, ALU.add).then_inc(x1_ready[t], 1)
                    for t in range(NT):
                        dve.wait_ge(x1_ready[t], this - 1)
                        last = dve.bn_stats(st_1[:, t, :], x1[:, t, :])
                    last.then_inc(bn_1_done, 1)
                    if older:
                        dve.wait_ge(y_ready[1], this - 2)
                    dve.wait_ge(dn_ready, this - 1)
                    dve.wait_ge(bn_1_done, this - 1)
                    dve.tensor_copy(d[:], dn[:]).then_inc(d_ready, 1)
                    for t in range(NT):
                        last = dve.bn_aggr(mv_1[:, t, :], st_1[:, t, :])
                    last.then_inc(mv_1_done, 1)
                    dve.wait_ge(mv_1_done, this - 1)
                    dve.tensor_scalar(ve_1[:], mv_1[:, :, 1], EPS, None, ALU.add).then_inc(ve_1_done, 1)
                    dve.wait_ge(d_ready, this - 1)
                    dve.wait_ge(rs_1_done, this - 1)
                    dve.tensor_tensor(sc_1[:], rs_1[:], d[:], ALU.mult).then_inc(sc_1_done, 1)
                    dve.wait_ge(sc_1_done, this - 1)
                    dve.scalar_tensor_tensor(nb_1[:], mv_1[:, :, 0], -1.0, sc_1[:], ALU.mult,
                                             ALU.mult).then_inc(ln_1_ready, 1)
                    for t in range(NT):
                        dve.wait_ge(h1_ready[t], this - 1)
                        dve.tensor_tensor(h1_lo[:, t, :], h1[:, t, :], h1_hi[:, t, :].bitcast(fp32),
                                          ALU.subtract).then_inc(h1_lo_ready[t], 1)
                if main:
                    for j in range(2):
                        dve.wait_ge(g_hi_ready[j], this)
                        for m in range(2 * j, 2 * j + 2):
                            last = dve.scalar_tensor_tensor(
                                g_lo[:, m, :], ps[:, G + j, m % 2 * N:m % 2 * N + N], u_col[:, m:m + 1],
                                g_hi[:, m, :].bitcast(fp32), ALU.add, ALU.subtract)
                        last.then_inc(g_lo_ready[j], 1)
                if ahead:
                    dve.wait_ge(x_loaded, (this + 1) * 16)
                    for t in range(NT):
                        last = dve.bn_stats(st_x[:, t, :], x_in[:, t, :])
                    last.then_inc(bn_x_done, 1)
                    dve.wait_ge(bn_x_done, this + 1)
                    if main:
                        value_low(0, this)
                    for t in range(NT):
                        last = dve.bn_aggr(mv_x[:, t, :], st_x[:, t, :])
                    last.then_inc(mv_x_done, 1)
                    dve.wait_ge(mv_x_done, this + 1)
                    dve.tensor_scalar(ve_x[:], mv_x[:, :, 1], EPS, None, ALU.add).then_inc(ve_x_done, 1)
                    if main:
                        value_low(1, this)
                    dve.wait_ge(rs_x_done, this + 1)
                    dve.scalar_tensor_tensor(nb_x[:], mv_x[:, :, 0], -1.0, rs_x[:], ALU.mult,
                                             ALU.mult).then_inc(ln_x_ready, 1)
                    if not main:
                        split_weights()
                elif main:
                    value_low(0, this)
                    value_low(1, this)
                if prev:
                    for j in range(2):
                        dve.wait_ge(z_hi_ready[j], this - 1)
                        dve.tensor_tensor(z_lo[:, 2 * j:2 * j + 2, :].rearrange("p c n -> p (c n)"),
                                          ps[:, Z + j, :],
                                          z_hi[:, 2 * j:2 * j + 2, :].rearrange("p c n -> p (c n)").bitcast(fp32),
                                          ALU.subtract).then_inc(z_lo_ready[j], 1)
                    for t in range(NT):
                        dve.scalar_tensor_tensor(x1b[:, t, :], b_row[:], sd[:, t:t + 1], x1[:, t, :],
                                                 ALU.mult, ALU.add).then_inc(x1b_ready[t], 1)
                if main:
                    dve.wait_ge(dr_done, this)
                    if prev:
                        dve.wait_ge(x1b_ready[1], this - 1)
                    for t in range(NT):
                        last = dve.tensor_tensor_reduce(
                            out=unused_a[:, t, :], in0=adj_kept[:, t, :], in1=ps[:, DR, 0:N], scale=1.0,
                            scalar=dn[:, t:t + 1], op0=ALU.mult, op1=ALU.add, accum_out=s_sum[:, t:t + 1])
                    last.then_inc(s_sum_ready, 1)
                    dve.wait_ge(s_sum_ready, this)
                    dve.tensor_tensor(sd[:], s_sum[:], dn[:], ALU.mult).then_inc(sd_ready, 1)
                    dve.wait_ge(adjt_ready, this)
                    for t in range(NT):
                        dve.wait_ge(e_ready[t], this)
                        dve.tensor_tensor(p[:, t, :], e[:, t, :], adjt[:, t, :], ALU.mult).then_inc(p_ready[t], 1)
                if ahead:
                    for t in range(NT):
                        dve.wait_ge(h_ready[t], this + 1)
                        dve.tensor_tensor_reduce(out=unused_h[:, t, :], in0=h[:, t, :], in1=c_row[:], scale=1.0,
                                                 scalar=bb_col[:, 0:1], op0=ALU.mult, op1=ALU.add,
                                                 accum_out=vk[:, t:t + 1]).then_inc(vk_ready[t], 1)
                if main:
                    for t in range(NT):
                        dve.wait_ge(p_hi_ready[t], this)
                        dve.tensor_tensor(p_lo[:, t, :], p[:, t, :], p_hi[:, t, :].bitcast(fp32),
                                          ALU.subtract).then_inc(p_lo_ready[t], 1)
                if ahead:
                    for j in range(2):
                        dve.wait_ge(ht_hi_ready[j], this + 1)
                        dve.tensor_tensor(ht_lo[:, 2 * j:2 * j + 2, :].rearrange("p c n -> p (c n)"),
                                          ps[:, HT + j, :],
                                          ht_hi[:, 2 * j:2 * j + 2, :].rearrange("p c n -> p (c n)").bitcast(fp32),
                                          ALU.subtract).then_inc(ht_lo_ready[j], 1)
                if prev:
                    if older:
                        dve.wait_ge(stored, (this - 2) * (16 * NT))
                    for t in range(NT):
                        dve.wait_ge(o1_done[t], this - 1)
                        dve.wait_ge(x1b_ready[t], this - 1)
                        dve.scalar_tensor_tensor(y[:, t, :], ps[:, O1 + t, :], d[:, t:t + 1], x1b[:, t, :],
                                                 ALU.mult, ALU.add).then_inc(y_ready[t], 1)

            steps(dve, step)

        @block.tensor
        def _(pe):
            def product(dst, pairs, cols):
                n = 0
                for stationary, moving in pairs:
                    for c in range(cols):
                        last = pe.matmul(dst, stationary(c), moving(c), start=(n == 0),
                                         stop=(n == len(pairs) * cols - 1))
                        n += 1
                return last

            def weights():
                pe.wait_ge(wv_loaded, 16)
                for c in range(DC):
                    for o in range(DC):
                        last = pe.transpose(ps[:, 4 + c, o * P:(o + 1) * P], wv_in[:, o, c * P:(c + 1) * P], ident[:])
                    last.then_inc(wvt_done, 1)
                pe.wait_ge(wqk_loaded, 32)
                for c in range(DC):
                    product(ps[:, c, :], [(lambda o, c=c: wk_in[:, o, c * P:(c + 1) * P], lambda o: wq_in[:, o, :])],
                            DC).then_inc(m_done, 1)
                pe.wait_ge(biases_loaded, 64)
                pe.wait_ge(consts_ready, 1)
                pe.wait_ge(bq_wide_ready, 1)
                pe.wait_ge(wvt_lo_ready, DC)
                pe.matmul(ps[:, 4, :], ones[0:1, :], bv_in[:], start=True, stop=True)
                pe.matmul(ps[:, 5, :], ones[0:1, :], b_in[:], start=True, stop=True)
                product(ps[:, 6, :], [(lambda o: bq_wide[:, o, :], lambda o: wk_in[:, o, :])], DC)
                for m in range(DC):
                    product(ps[:, 7, m:m + 1], [(lambda o, m=m: wq_in[:, o, m * P:(m + 1) * P],
                                                 lambda o: bk_col[:, o:o + 1])], DC)
                product(ps[:, 7, DC:DC + 1], [(lambda o: bq_wide[:, o, :], lambda o: bk_col[:, o:o + 1])],
                        DC).then_inc(rows_done, 1)
                pe.wait_ge(rows_ready, 1)
                pe.wait_ge(m_lo_ready, DC)

            def step(this, prev, main, ahead, older=True):
                if main:
                    pe.wait_ge(ht_lo_ready[0], this)
                    pe.wait_ge(ht_lo_ready[1], this)
                    for m in range(DC):
                        cols = slice(m * P, (m + 1) * P)
                        last = product(ps[:, G + m // 2, m % 2 * N:m % 2 * N + N],
                                       [(lambda c: m_hi[:, c, cols], lambda c: ht_hi[:, c, :]),
                                        (lambda c: m_hi[:, c, cols], lambda c: ht_lo[:, c, :]),
                                        (lambda c: m_lo[:, c, cols], lambda c: ht_hi[:, c, :])], DC)
                        if m % 2:
                            last.then_inc(g_done[m // 2], 1)
                if main:
                    for t in range(NT):
                        if prev and older:
                            pe.wait_ge(y_ready[t], this - 2)
                        cols = slice(t * P, (t + 1) * P)
                        product(ps[:, V + t, :],
                                [(lambda c: ht_hi[:, c, cols], lambda c: wvt_hi[:, c, :]),
                                 (lambda c: ht_hi[:, c, cols], lambda c: wvt_lo[:, c, :]),
                                 (lambda c: ht_lo[:, c, cols], lambda c: wvt_hi[:, c, :])],
                                DC).then_inc(v_done[t], 1)
                if prev:
                    pe.wait_ge(hat_lo_ready, this - 1)
                    pe.wait_ge(h1_lo_ready[0], this - 1)
                    pe.wait_ge(h1_lo_ready[1], this - 1)
                    for m in range(DC):
                        cols = slice(m * P, (m + 1) * P)
                        last = product(ps[:, Z + m // 2, m % 2 * N:m % 2 * N + N],
                                       [(lambda c: h1_hi[:, c, cols], lambda c: hat_hi[:, c, :]),
                                        (lambda c: h1_hi[:, c, cols], lambda c: hat_lo[:, c, :]),
                                        (lambda c: h1_lo[:, c, cols], lambda c: hat_hi[:, c, :])], NT)
                        if m % 2:
                            last.then_inc(z_done[m // 2], 1)
                if main:
                    pe.wait_ge(dn_ready, this)
                    if prev:
                        pe.wait_ge(x1_ready[0], this - 1)
                    for t in range(NT):
                        last = pe.transpose(ps[:, DR, t * P:(t + 1) * P], dn[:, t:t + 1].to_broadcast([P, P]), ident[:])
                    last.then_inc(dr_done, 1)
                    pe.wait_ge(g_lo_ready[0], this)
                    pe.wait_ge(g_lo_ready[1], this)
                    for t in range(NT):
                        cols = slice(t * P, (t + 1) * P)
                        product(ps[:, G + t, 0:N],
                                [(lambda c: g_hi[:, c, cols], lambda c: ht_hi[:, c, :]),
                                 (lambda c: g_hi[:, c, cols], lambda c: ht_lo[:, c, :]),
                                 (lambda c: g_lo[:, c, cols], lambda c: ht_hi[:, c, :])],
                                DC).then_inc(s_done[t], 1)
                if ahead:
                    if not main:
                        pe.wait_ge(ident_ready, 1)
                        weights()
                    pe.wait_ge(adj_loaded, (this + 1) * 16)
                    for k in range(NT):
                        for q in range(NT):
                            last = pe.transpose(ps[:, AT, k * N + q * P:k * N + (q + 1) * P],
                                                adj_in[:, q, k * P:(k + 1) * P], ident[:])
                    last.then_inc(at_done, 1)
                    pe.wait_ge(h_ready[0], this + 1)
                    pe.wait_ge(h_ready[1], this + 1)
                    for c in range(DC):
                        if prev and c % 2 == 0:
                            pe.wait_ge(z_lo_ready[c // 2], this - 1)
                        for t in range(NT):
                            last = pe.transpose(ps[:, HT + c // 2, c % 2 * N + t * P:c % 2 * N + (t + 1) * P],
                                                h[:, t, c * P:(c + 1) * P], ident[:])
                        if c % 2:
                            last.then_inc(ht_done[c // 2], 1)
                if prev:
                    pe.wait_ge(w_lo_ready, 1)
                    pe.wait_ge(z_lo_ready[0], this - 1)
                    pe.wait_ge(z_lo_ready[1], this - 1)
                    for t in range(NT):
                        if main:
                            pe.wait_ge(v_lo_ready[t], this)
                        cols = slice(t * P, (t + 1) * P)
                        product(ps[:, O1 + t, :],
                                [(lambda c: z_hi[:, c, cols], lambda c: w_hi[:, c, :]),
                                 (lambda c: z_hi[:, c, cols], lambda c: w_lo[:, c, :]),
                                 (lambda c: z_lo[:, c, cols], lambda c: w_hi[:, c, :])],
                                DC).then_inc(o1_done[t], 1)
                if main:
                    pe.wait_ge(p_lo_ready[0], this)
                    pe.wait_ge(p_lo_ready[1], this)
                    pe.wait_ge(consts_ready, 2)
                    pe.wait_ge(v_lo_ready[0], this)
                    pe.wait_ge(v_lo_ready[1], this)
                    pe.wait_ge(s_sum_ready, this)
                    if ahead:
                        pe.wait_ge(adjt_ready, this + 1)
                    for t in range(NT):
                        if ahead and t:
                            pe.wait_ge(ht_lo_ready[0], this + 1)
                            pe.wait_ge(ht_lo_ready[1], this + 1)
                        cols = slice(t * P, (t + 1) * P)
                        for a, width in enumerate((HD + 2, HD)):
                            last = product(ps[:, O[t] + a, 0:width],
                                           [(lambda c: p_hi[:, c, cols], lambda c: v_hi[:, c, a, 0:width]),
                                            (lambda c: p_hi[:, c, cols], lambda c: v_lo[:, c, a, 0:width]),
                                            (lambda c: p_lo[:, c, cols], lambda c: v_hi[:, c, a, 0:width])], NT)
                        last.then_inc(o_done[t], 1)

            steps(pe, step)


_INS = ["x", "adj", "L0_gnn_Wq_w", "L0_gnn_Wq_b", "L0_gnn_Wk_w", "L0_gnn_Wk_b", "L0_gnn_Wv_w", "L0_gnn_Wv_b",
        "L1_gnn_W", "L1_gnn_b"]


def kernel(**inputs):
    import numpy as _np
    import concourse.bacc as _bacc
    from concourse import mybir as _mybir
    from concourse.bass_utils import run_bass_kernel_spmd as _run

    nc = _bacc.Bacc("TRN2", target_bir_lowering=False, num_devices=1)
    arrays, args = {}, []
    for name in _INS:
        a = _np.ascontiguousarray(inputs[name])
        arrays[f"in_{name}_dram"] = a
        args.append(nc.dram_tensor(f"in_{name}_dram", a.shape, _mybir.dt.from_np(a.dtype), kind="ExternalInput").ap())
    out = nc.dram_tensor("out_dram", (B, N, D), _mybir.dt.float32, kind="ExternalOutput").ap()
    gnn_program(nc, *args, out)
    r = _run(nc, [arrays], core_ids=[0])
    return r.results[0]["out_dram"]
```

```python
import concourse.bass as bass
from concourse import mybir
from contextlib import ExitStack

B, N, D = 64, 256, 512
P = 128
NT = N // P
DC = D // P
HD = D // 2
EPS = 1e-5


def gnn_program(nc, x, adj, wq, bq, wk, bk, wv, bv, w, b, out):
    fp32, f32r = mybir.dt.float32, mybir.dt.float32r
    ALU, ACT, AX = mybir.AluOpType, mybir.ActivationFunctionType, mybir.AxisListType

    ctx = ExitStack()
    with ctx:
        def sb(name, shape, dt=fp32):
            return ctx.enter_context(nc.sbuf_tensor(name, shape, dt))

        def sem(name):
            return ctx.enter_context(nc.semaphore(name))

        def sems(name, n=2):
            return [sem(f"{name}{k}") for k in range(n)]

        m_hi, m_lo = sb("m_hi", [P, DC, D], f32r), sb("m_lo", [P, DC, D], f32r)
        wvt_hi, wvt_lo = sb("wvt_hi", [P, DC, D], f32r), sb("wvt_lo", [P, DC, D], f32r)
        w_hi, w_lo = sb("w_hi", [P, DC, D], f32r), sb("w_lo", [P, DC, D], f32r)
        u_col = sb("u_col", [P, DC])
        c_row = sb("c_row", [P, D])
        bb_col = sb("bb_col", [P, 1])
        bv_row, b_row = sb("bv_row", [P, D]), sb("b_row", [P, D])
        ident = sb("ident", [P, P])
        eye = sb("eye", [P, NT, N])
        ones = sb("ones", [P, P])
        minus_half = sb("minus_half", [P, NT])
        bq_col, bk_col = sb("bq_col", [P, DC]), sb("bk_col", [P, DC])
        c_part, u_part, bb_part, bb_out = sb("c_part", [P, D]), sb("u_part", [P, D]), sb("bb_part", [P, 1]), sb("bb_out", [P, DC])

        x_in = sb("x_in", [P, NT, D])
        adj_in = sb("adj_in", [P, NT, N])
        h = sb("h", [P, NT, D])
        ht_hi, ht_lo = sb("ht_hi", [P, DC, N], f32r), sb("ht_lo", [P, DC, N], f32r)
        g_hi, g_lo = sb("g_hi", [P, DC, N], f32r), sb("g_lo", [P, DC, N], f32r)
        adjt = sb("adjt", [P, NT, N])
        e = sb("e", [P, NT, N])
        p = sb("p", [P, NT, N])
        p_hi, p_lo = sb("p_hi", [P, NT, N], f32r), sb("p_lo", [P, NT, N], f32r)
        v_hi, v_lo = sb("v_hi", [P, NT, 2, HD + 2], f32r), sb("v_lo", [P, NT, 2, HD + 2], f32r)
        xb = sb("xb", [P, NT, D])
        hat = sb("hat", [P, NT, N])
        hat_hi, hat_lo = sb("hat_hi", [P, NT, N], f32r), sb("hat_lo", [P, NT, N], f32r)
        h1_hi, h1_lo = sb("h1_hi", [P, NT, D], f32r), sb("h1_lo", [P, NT, D], f32r)
        z_hi, z_lo = sb("z_hi", [P, DC, N], f32r), sb("z_lo", [P, DC, N], f32r)
        late = sb("late", [P, 4, NT * D])
        wq_in = late[:, 0:2, :].rearrange("p a (c d) -> p (a c) d", d=D)
        wk_in = late[:, 2:4, :].rearrange("p a (c d) -> p (a c) d", d=D)
        x1, h1, x1b, y = (late[:, k, :].rearrange("p (t d) -> p t d", t=NT) for k in range(4))
        wv_in, w_in = sb("wv_in", [P, DC, D]), sb("w_in", [P, DC, D])
        adj_kept = w_in[:, 0, :].rearrange("p (t n) -> p t n", t=NT)
        unused_h = w_in[:, 1:1 + NT, :]
        unused_a = w_in[:, 3, :].rearrange("p (t n) -> p t n", t=NT)

        st_x, st_1 = sb("st_x", [P, NT, 6]), sb("st_1", [P, NT, 6])
        mv_x, mv_1 = sb("mv_x", [P, NT, 2]), sb("mv_1", [P, NT, 2])
        ve_x, ve_1 = sb("ve_x", [P, NT]), sb("ve_1", [P, NT])
        rs_x, rs_1 = sb("rs_x", [P, NT]), sb("rs_1", [P, NT])
        sc_1 = sb("sc_1", [P, NT])
        nb_x, nb_1 = sb("nb_x", [P, NT]), sb("nb_1", [P, NT])
        vk = sb("vk", [P, NT])
        rsum, rsum1 = sb("rsum", [P, NT]), sb("rsum1", [P, NT])
        dn, d = sb("dn", [P, NT]), sb("d", [P, NT])
        rinv = sb("rinv", [P, NT])
        s_sum, sd = sb("s_sum", [P, NT]), sb("sd", [P, NT])

        ps = ctx.enter_context(nc.psum_tensor("ps", [P, 8, 512], fp32))
        G, Z, HT, V, O1, AT, DR = 0, 2, 2, 4, 4, 6, 7
        O = (6, 2)
        W_BANKS = (0, 1, 4, 5)
        C_BANK, U_BANK = 7, 6

        consts_ready, ident_ready = sem("consts_ready"), sem("ident_ready")
        ident_zero = sem("ident_zero")
        wqk_loaded, wv_loaded, w_loaded = sems("wqk_loaded", DC), sem("wv_loaded"), sem("w_loaded")
        columns_loaded, bias_rows_loaded = sem("columns_loaded"), sem("bias_rows_loaded")
        m_done, wvt_done = sem("m_done"), sem("wvt_done")
        m_hi_ready, m_lo_ready = sem("m_hi_ready"), sem("m_lo_ready")
        wvt_hi_ready, wvt_lo_ready = sem("wvt_hi_ready"), sem("wvt_lo_ready")
        w_hi_ready, w_lo_ready = sem("w_hi_ready"), sem("w_lo_ready")
        parts_ready, bb_part_ready = sem("parts_ready"), sem("bb_part_ready")
        c_done, u_done, c_ready, u_ready = sem("c_done"), sem("u_done"), sem("c_ready"), sem("u_ready")

        x_loaded, adj_loaded, stored = sem("x_loaded"), sem("adj_loaded"), sem("stored")
        bn_x_done, mv_x_done, ve_x_done, rs_x_done, ln_x_ready = (
            sem("bn_x_done"), sem("mv_x_done"), sem("ve_x_done"), sem("rs_x_done"), sem("ln_x_ready"))
        bn_1_done, mv_1_done, ve_1_done, rs_1_done, sc_1_done, ln_1_ready = (
            sem("bn_1_done"), sem("mv_1_done"), sem("ve_1_done"), sem("rs_1_done"), sem("sc_1_done"),
            sem("ln_1_ready"))
        h_ready = sems("h_ready")
        rsum_ready, rsum1_ready, dn_ready, d_ready = (
            sem("rsum_ready"), sem("rsum1_ready"), sem("dn_ready"), sem("d_ready"))
        at_done, adjt_ready = sem("at_done"), sem("adjt_ready")
        ht_done, ht_hi_ready, ht_lo_ready = sems("ht_done"), sems("ht_hi_ready"), sems("ht_lo_ready")
        vk_ready = sems("vk_ready")
        g_done, g_hi_ready, g_lo_ready = sems("g_done"), sems("g_hi_ready"), sems("g_lo_ready")
        v_done, v_hi_ready, v_lo_ready = sems("v_done"), sems("v_hi_ready"), sems("v_lo_ready")
        s_done, e_ready, p_ready = sems("s_done"), sems("e_ready"), sems("p_ready")
        p_hi_ready, p_lo_ready = sems("p_hi_ready"), sems("p_lo_ready")
        rinv_ready, o_done = sems("rinv_ready"), sems("o_done")
        xb_ready, x1_ready = sem("xb_ready"), sems("x1_ready")
        hat_hi_ready, hat_ready, hat_lo_ready = sem("hat_hi_ready"), sem("hat_ready"), sem("hat_lo_ready")
        h1_ready, h1_lo_ready = sems("h1_ready"), sems("h1_lo_ready")
        z_done, z_hi_ready, z_lo_ready = sems("z_done"), sems("z_hi_ready"), sems("z_lo_ready")
        dr_done, s_sum_ready, sd_ready, x1b_ready = (
            sem("dr_done"), sem("s_sum_ready"), sem("sd_ready"), sems("x1b_ready"))
        o1_done, y_ready = sems("o1_done"), sems("y_ready")

        block = ctx.enter_context(nc.Block())

        def halves(row):
            return row.rearrange("p (a n) -> p a n", a=2)

        def steps(eng, step):
            step(0, prev=False, main=False, ahead=True)
            step(1, prev=False, main=True, ahead=True)
            step(2, prev=True, main=True, ahead=True, older=False)
            with eng.Fori(3, B) as this:
                step(this, prev=True, main=True, ahead=True)
            step(B, prev=True, main=True, ahead=False)
            step(B + 1, prev=True, main=False, ahead=False)


        @block.sync
        def _(sp):
            for o in range(DC):
                sp.dma_start(wk_in[:, o, :], wk[o * P:(o + 1) * P, :]).then_inc(wqk_loaded[o], 16)
            sp.dma_start(x_in[:], x[0].rearrange("(t p) d -> p t d", p=P)).then_inc(x_loaded, 16)
            sp.dma_start(adj_in[:], adj[0].rearrange("(t p) n -> p t n", p=P)).then_inc(adj_loaded, 16)
            sp.dma_start(wv_in[:], wv.rearrange("(c p) d -> p c d", p=P)).then_inc(wv_loaded, 16)
            sp.dma_start(w_in[:], w.rearrange("(c p) d -> p c d", p=P)).then_inc(w_loaded, 16)

            adj_flat, x_flat = adj.rearrange("g n m -> (g n m)"), x.rearrange("g n d -> (g n d)")

            def step(this, prev, main, ahead, older=True):
                if main and ahead:
                    adj_next = adj_flat[bass.ds(sp.snap(this * (N * N)), N * N)]
                    x_next = x_flat[bass.ds(sp.snap(this * (N * D)), N * D)]
                    sp.wait_ge(at_done, this)
                    sp.wait_ge(rsum_ready, this)
                    sp.dma_start(adj_in[:], adj_next.rearrange("(t p n) -> p t n", p=P, n=N)).then_inc(adj_loaded, 16)
                    sp.wait_ge(h_ready[1], this)
                    sp.wait_ge(xb_ready, this)
                    sp.dma_start(x_in[:], x_next.rearrange("(t p d) -> p t d", p=P, d=D)).then_inc(x_loaded, 16)
                if prev:
                    for t in range(NT):
                        sp.wait_ge(y_ready[t], this - 1)
                        sp.dma_start(out[this - 2, t * P:(t + 1) * P, :], y[:, t, :]).then_inc(stored, 16)

            steps(sp, step)
            sp.wait_ge(stored, B * 16 * NT)

        @block.gpsimd
        def _(pool):
            pool.memset(ident[:], 0.0)
            pool.memset(eye[:], 0.0).then_inc(ident_zero, 1)
            pool.wait_ge(ident_zero, 1)
            pool.affine_select(out=ident[:], in_=ident[:], compare_op=ALU.not_equal, fill=1.0,
                               base=0, pattern=[[-1, P]], channel_multiplier=1).then_inc(ident_ready, 1)
            pool.affine_select(out=eye[:], in_=eye[:], compare_op=ALU.not_equal, fill=1.0, base=0,
                               pattern=[[P, NT], [-1, N]], channel_multiplier=1)
            pool.memset(minus_half[:], -0.5).then_inc(ident_ready, 1)
            pool.wait_ge(consts_ready, 1)
            pool.wait_ge(ident_ready, 2)

            def step(this, prev, main, ahead, older=True):
                if main:
                    if not prev:
                        pool.wait_ge(bias_rows_loaded, 32)
                    pool.wait_ge(x_loaded, this * 16)
                    for t in range(NT):
                        if prev:
                            pool.wait_ge(x1_ready[t], this - 1)
                        last = pool.tensor_tensor(xb[:, t, :], x_in[:, t, :], bv_row[:], ALU.add)
                    last.then_inc(xb_ready, 1)
                if prev:
                    pool.wait_ge(ve_1_done, this - 1)
                    pool.tensor_tensor(rs_1[:], ve_1[:], minus_half[:], ALU.pow).then_inc(rs_1_done, 1)
                if main:
                    if prev:
                        pool.wait_ge(d_ready, this - 1)
                    pool.wait_ge(rsum_ready, this)
                    pool.tensor_tensor(rsum1[:], rsum[:], ones[:, 0:NT], ALU.add).then_inc(rsum1_ready, 1)
                    pool.wait_ge(rsum1_ready, this)
                    pool.tensor_tensor(dn[:], rsum1[:], minus_half[:], ALU.pow).then_inc(dn_ready, 1)
                if ahead:
                    pool.wait_ge(ve_x_done, this + 1)
                    pool.tensor_tensor(rs_x[:], ve_x[:], minus_half[:], ALU.pow).then_inc(rs_x_done, 1)
                if main:
                    pool.wait_ge(adjt_ready, this)
                    if prev:
                        pool.wait_ge(z_done[1], this - 1)
                    pool.tensor_tensor(hat_hi[:], adjt[:], eye[:], ALU.add).then_inc(hat_hi_ready, 1)
                    pool.tensor_tensor(hat[:], adjt[:], eye[:], ALU.add).then_inc(hat_ready, 1)
                    pool.wait_ge(hat_ready, this)
                    pool.tensor_tensor(hat_lo[:], hat[:], hat_hi[:].bitcast(fp32), ALU.subtract).then_inc(hat_lo_ready, 1)

            steps(pool, step)

        @block.scalar
        def _(act):
            act.dma_start(bq_col[:], bq.rearrange("(c p) -> p c", p=P),
                          allow_slow_non_contiguous=True).then_inc(columns_loaded, 16)
            act.dma_start(bk_col[:], bk.rearrange("(c p) -> p c", p=P),
                          allow_slow_non_contiguous=True).then_inc(columns_loaded, 16)
            for o in range(DC):
                act.dma_start(wq_in[:, o, :], wq[o * P:(o + 1) * P, :]).then_inc(wqk_loaded[o], 16)
            act.dma_start(bv_row[:], bv.partition_broadcast(P)).then_inc(bias_rows_loaded, 16)
            act.dma_start(b_row[:], b.partition_broadcast(P)).then_inc(bias_rows_loaded, 16)

            def m_high():
                for c in range(DC):
                    act.wait_ge(m_done, c + 1)
                    act.activation(m_hi[:, c, :], ps[:, W_BANKS[c], :], ACT.Copy).then_inc(m_hi_ready, 1)

            def wv_and_w_high():
                for c in range(DC):
                    act.wait_ge(wvt_done, c + 1)
                    act.activation(wvt_hi[:, c, :], ps[:, W_BANKS[c], :], ACT.Copy).then_inc(wvt_hi_ready, 1)
                act.wait_ge(w_loaded, 16)
                act.activation(w_hi[:], w_in[:], ACT.Copy).then_inc(w_hi_ready, 1)

            def value_high(t, this):
                act.wait_ge(v_done[t], this)
                act.activation(v_hi[:, t, :, 0:HD], halves(ps[:, V + t, :]), ACT.Copy).then_inc(v_hi_ready[t], 1)

            def step(this, prev, main, ahead, older=True):
                if prev:
                    act.wait_ge(ln_1_ready, this - 1)
                    for t in range(NT):
                        act.activation(h1[:, t, :], x1[:, t, :], ACT.Relu, scale=sc_1[:, t:t + 1],
                                       bias=nb_1[:, t:t + 1])
                        act.activation(h1_hi[:, t, :], x1[:, t, :], ACT.Relu, scale=sc_1[:, t:t + 1],
                                       bias=nb_1[:, t:t + 1]).then_inc(h1_ready[t], 1)
                if main:
                    if not prev:
                        act.wait_ge(u_ready, 1)
                    for j in range(2):
                        act.wait_ge(g_done[j], this)
                        for m in range(2 * j, 2 * j + 2):
                            last = act.activation(g_hi[:, m, :], ps[:, G + j, m % 2 * N:m % 2 * N + N],
                                                  ACT.Identity, bias=u_col[:, m:m + 1])
                        last.then_inc(g_hi_ready[j], 1)
                if main:
                    value_high(0, this)
                    value_high(1, this)
                if ahead:
                    act.wait_ge(ln_x_ready, this + 1)
                    for t in range(NT):
                        act.activation(h[:, t, :], x_in[:, t, :], ACT.Relu, scale=rs_x[:, t:t + 1],
                                       bias=nb_x[:, t:t + 1]).then_inc(h_ready[t], 1)
                    if not main:
                        m_high()
                if prev:
                    for j in range(2):
                        act.wait_ge(z_done[j], this - 1)
                        act.activation(z_hi[:, 2 * j:2 * j + 2, :].rearrange("p c n -> p (c n)"),
                                       ps[:, Z + j, :], ACT.Copy).then_inc(z_hi_ready[j], 1)
                if main:
                    for t in range(NT):
                        act.wait_ge(s_done[t], this)
                        act.wait_ge(vk_ready[t], this)
                        act.activation(e[:, t, :], ps[:, G + t, 0:N], ACT.Exp,
                                       bias=vk[:, t:t + 1]).then_inc(e_ready[t], 1)
                    for t in range(NT):
                        act.wait_ge(p_ready[t], this)
                        act.activation(p_hi[:, t, :], p[:, t, :], ACT.Copy).then_inc(p_hi_ready[t], 1)
                if ahead:
                    act.wait_ge(at_done, this + 1)
                    if main:
                        act.wait_ge(hat_ready, this)
                    act.activation(adjt[:].rearrange("p t n -> p (t n)"), ps[:, AT, :],
                                   ACT.Copy).then_inc(adjt_ready, 1)
                    for j in range(2):
                        act.wait_ge(ht_done[j], this + 1)
                        act.activation(ht_hi[:, 2 * j:2 * j + 2, :].rearrange("p c n -> p (c n)"),
                                       ps[:, HT + j, :], ACT.Copy).then_inc(ht_hi_ready[j], 1)
                    if not main:
                        wv_and_w_high()
                    act.wait_ge(adj_loaded, (this + 1) * 16)
                    if main:
                        act.wait_ge(sd_ready, this)
                    else:
                        act.wait_ge(w_lo_ready, 1)
                    for t in range(NT):
                        last = act.activation(adj_kept[:, t, :], adj_in[:, t, :], ACT.Copy,
                                              accum_out=rsum[:, t:t + 1])
                    last.then_inc(rsum_ready, 1)

            steps(act, step)

        @block.vector
        def _(dve):
            dve.memset(ones[:], 1.0).then_inc(consts_ready, 1)
            dve.wait_ge(consts_ready, 1)
            dve.tensor_copy(v_hi[:, :, 0, HD:HD + 2], ones[:, 0:2 * NT].rearrange("p (t a) -> p t a", t=NT))
            dve.tensor_scalar(v_lo[:, :, 0, HD:HD + 2], ones[:, 0:2 * NT].rearrange("p (t a) -> p t a", t=NT),
                              0.0, None, ALU.mult).then_inc(consts_ready, 1)
            dve.wait_ge(columns_loaded, 32)
            dve.tensor_tensor_reduce(out=bb_out[:], in0=bq_col[:], in1=bk_col[:], scale=1.0, scalar=0.0,
                                     op0=ALU.mult, op1=ALU.add, accum_out=bb_part[:]).then_inc(bb_part_ready, 1)
            for o in range(DC):
                dve.wait_ge(wqk_loaded[o], 32)
                if o == 0:
                    dve.tensor_scalar(c_part[:], wk_in[:, o, :], bq_col[:, o:o + 1], None, ALU.mult)
                    dve.tensor_scalar(u_part[:], wq_in[:, o, :], bk_col[:, o:o + 1], None,
                                      ALU.mult).then_inc(parts_ready, 1)
                else:
                    dve.wait_ge(parts_ready, o)
                    dve.scalar_tensor_tensor(c_part[:], wk_in[:, o, :], bq_col[:, o:o + 1], c_part[:],
                                             ALU.mult, ALU.add)
                    dve.scalar_tensor_tensor(u_part[:], wq_in[:, o, :], bk_col[:, o:o + 1], u_part[:],
                                             ALU.mult, ALU.add).then_inc(parts_ready, 1)

            def m_low():
                for c in range(DC):
                    dve.wait_ge(m_hi_ready, c + 1)
                    dve.tensor_tensor(m_lo[:, c, :], ps[:, W_BANKS[c], :], m_hi[:, c, :].bitcast(fp32),
                                      ALU.subtract).then_inc(m_lo_ready, 1)

            def bias_products():
                dve.wait_ge(c_done, 1)
                dve.tensor_copy(c_row[:], ps[:, C_BANK, :]).then_inc(c_ready, 1)
                dve.wait_ge(u_done, 1)
                dve.tensor_copy(u_col[:], ps[:, U_BANK, 0:DC])
                dve.tensor_copy(bb_col[:], ps[:, U_BANK, DC:DC + 1]).then_inc(u_ready, 1)
                dve.wait_ge(c_ready, 1)
                dve.wait_ge(u_ready, 1)

            def wv_and_w_low():
                for c in range(DC):
                    dve.wait_ge(wvt_hi_ready, c + 1)
                    dve.tensor_tensor(wvt_lo[:, c, :], ps[:, W_BANKS[c], :], wvt_hi[:, c, :].bitcast(fp32),
                                      ALU.subtract).then_inc(wvt_lo_ready, 1)
                dve.wait_ge(w_hi_ready, 1)
                dve.tensor_tensor(w_lo[:], w_in[:], w_hi[:].bitcast(fp32), ALU.subtract).then_inc(w_lo_ready, 1)
                dve.wait_ge(w_lo_ready, 1)

            def score_bias(this):
                for t in range(NT):
                    dve.wait_ge(h_ready[t], this)
                    dve.tensor_tensor_reduce(out=unused_h[:, t, :], in0=h[:, t, :], in1=c_row[:], scale=1.0,
                                             scalar=bb_col[:, 0:1], op0=ALU.mult, op1=ALU.add,
                                             accum_out=vk[:, t:t + 1]).then_inc(vk_ready[t], 1)

            def value_low(t, this):
                dve.wait_ge(v_hi_ready[t], this)
                dve.tensor_tensor(v_lo[:, t, :, 0:HD], halves(ps[:, V + t, :]), v_hi[:, t, :, 0:HD].bitcast(fp32),
                                  ALU.subtract).then_inc(v_lo_ready[t], 1)

            def step(this, prev, main, ahead, older=True):
                if prev:
                    dve.wait_ge(xb_ready, this - 1)
                    for t in range(NT):
                        dve.wait_ge(o_done[t], this - 1)
                        dve.reciprocal(rinv[:, t:t + 1], ps[:, O[t], HD:HD + 1]).then_inc(rinv_ready[t], 1)
                        dve.wait_ge(rinv_ready[t], this - 1)
                        dve.scalar_tensor_tensor(halves(x1[:, t, :]), ps[:, O[t]:O[t] + 2, 0:HD], rinv[:, t:t + 1],
                                                 halves(xb[:, t, :]), ALU.mult, ALU.add).then_inc(x1_ready[t], 1)
                    for t in range(NT):
                        dve.wait_ge(x1_ready[t], this - 1)
                        last = dve.bn_stats(st_1[:, t, :], x1[:, t, :])
                    last.then_inc(bn_1_done, 1)
                    if older:
                        dve.wait_ge(y_ready[1], this - 2)
                    dve.wait_ge(dn_ready, this - 1)
                    dve.wait_ge(bn_1_done, this - 1)
                    dve.tensor_copy(d[:], dn[:]).then_inc(d_ready, 1)
                    for t in range(NT):
                        last = dve.bn_aggr(mv_1[:, t, :], st_1[:, t, :])
                    last.then_inc(mv_1_done, 1)
                    dve.wait_ge(mv_1_done, this - 1)
                    dve.tensor_scalar(ve_1[:], mv_1[:, :, 1], EPS, None, ALU.add).then_inc(ve_1_done, 1)
                    dve.wait_ge(d_ready, this - 1)
                    dve.wait_ge(rs_1_done, this - 1)
                    dve.tensor_tensor(sc_1[:], rs_1[:], d[:], ALU.mult).then_inc(sc_1_done, 1)
                    dve.wait_ge(sc_1_done, this - 1)
                    dve.scalar_tensor_tensor(nb_1[:], mv_1[:, :, 0], -1.0, sc_1[:], ALU.mult,
                                             ALU.mult).then_inc(ln_1_ready, 1)
                    for t in range(NT):
                        dve.wait_ge(h1_ready[t], this - 1)
                        dve.tensor_tensor(h1_lo[:, t, :], h1[:, t, :], h1_hi[:, t, :].bitcast(fp32),
                                          ALU.subtract).then_inc(h1_lo_ready[t], 1)
                if main:
                    for j in range(2):
                        dve.wait_ge(g_hi_ready[j], this)
                        for m in range(2 * j, 2 * j + 2):
                            last = dve.scalar_tensor_tensor(
                                g_lo[:, m, :], ps[:, G + j, m % 2 * N:m % 2 * N + N], u_col[:, m:m + 1],
                                g_hi[:, m, :].bitcast(fp32), ALU.add, ALU.subtract)
                        last.then_inc(g_lo_ready[j], 1)
                if ahead:
                    dve.wait_ge(x_loaded, (this + 1) * 16)
                    for t in range(NT):
                        last = dve.bn_stats(st_x[:, t, :], x_in[:, t, :])
                    last.then_inc(bn_x_done, 1)
                    dve.wait_ge(bn_x_done, this + 1)
                    if main:
                        value_low(0, this)
                    for t in range(NT):
                        last = dve.bn_aggr(mv_x[:, t, :], st_x[:, t, :])
                    last.then_inc(mv_x_done, 1)
                    dve.wait_ge(mv_x_done, this + 1)
                    dve.tensor_scalar(ve_x[:], mv_x[:, :, 1], EPS, None, ALU.add).then_inc(ve_x_done, 1)
                    if main:
                        value_low(1, this)
                    dve.wait_ge(rs_x_done, this + 1)
                    dve.scalar_tensor_tensor(nb_x[:], mv_x[:, :, 0], -1.0, rs_x[:], ALU.mult,
                                             ALU.mult).then_inc(ln_x_ready, 1)
                    if not main:
                        m_low()
                elif main:
                    value_low(0, this)
                    value_low(1, this)
                if prev:
                    for j in range(2):
                        dve.wait_ge(z_hi_ready[j], this - 1)
                        dve.tensor_tensor(z_lo[:, 2 * j:2 * j + 2, :].rearrange("p c n -> p (c n)"),
                                          ps[:, Z + j, :],
                                          z_hi[:, 2 * j:2 * j + 2, :].rearrange("p c n -> p (c n)").bitcast(fp32),
                                          ALU.subtract).then_inc(z_lo_ready[j], 1)
                    for t in range(NT):
                        dve.scalar_tensor_tensor(x1b[:, t, :], b_row[:], sd[:, t:t + 1], x1[:, t, :],
                                                 ALU.mult, ALU.add).then_inc(x1b_ready[t], 1)
                if main:
                    dve.wait_ge(dr_done, this)
                    if prev:
                        dve.wait_ge(x1b_ready[1], this - 1)
                    for t in range(NT):
                        last = dve.tensor_tensor_reduce(
                            out=unused_a[:, t, :], in0=adj_kept[:, t, :], in1=ps[:, DR, 0:N], scale=1.0,
                            scalar=dn[:, t:t + 1], op0=ALU.mult, op1=ALU.add, accum_out=s_sum[:, t:t + 1])
                    last.then_inc(s_sum_ready, 1)
                    dve.wait_ge(s_sum_ready, this)
                    dve.tensor_tensor(sd[:], s_sum[:], dn[:], ALU.mult).then_inc(sd_ready, 1)
                    dve.wait_ge(adjt_ready, this)
                    for t in range(NT):
                        dve.wait_ge(e_ready[t], this)
                        dve.tensor_tensor(p[:, t, :], e[:, t, :], adjt[:, t, :], ALU.mult).then_inc(p_ready[t], 1)
                if main and ahead:
                    score_bias(this + 1)
                if main:
                    for t in range(NT):
                        dve.wait_ge(p_hi_ready[t], this)
                        dve.tensor_tensor(p_lo[:, t, :], p[:, t, :], p_hi[:, t, :].bitcast(fp32),
                                          ALU.subtract).then_inc(p_lo_ready[t], 1)
                if ahead:
                    for j in range(2):
                        dve.wait_ge(ht_hi_ready[j], this + 1)
                        dve.tensor_tensor(ht_lo[:, 2 * j:2 * j + 2, :].rearrange("p c n -> p (c n)"),
                                          ps[:, HT + j, :],
                                          ht_hi[:, 2 * j:2 * j + 2, :].rearrange("p c n -> p (c n)").bitcast(fp32),
                                          ALU.subtract).then_inc(ht_lo_ready[j], 1)
                    if not main:
                        bias_products()
                        wv_and_w_low()
                        score_bias(this + 1)
                if prev:
                    if older:
                        dve.wait_ge(stored, (this - 2) * (16 * NT))
                    for t in range(NT):
                        dve.wait_ge(o1_done[t], this - 1)
                        dve.wait_ge(x1b_ready[t], this - 1)
                        dve.scalar_tensor_tensor(y[:, t, :], ps[:, O1 + t, :], d[:, t:t + 1], x1b[:, t, :],
                                                 ALU.mult, ALU.add).then_inc(y_ready[t], 1)

            steps(dve, step)

        @block.tensor
        def _(pe):
            def product(dst, chunks, a, cols, b):
                (a_hi, a_lo), (b_hi, b_lo) = a, b
                for c in range(chunks):
                    pe.matmul(dst, a_hi[:, c, cols], b_hi[:, c, :], start=(c == 0), stop=False)
                    pe.matmul(dst, a_hi[:, c, cols], b_lo[:, c, :], start=False, stop=False)
                    last = pe.matmul(dst, a_lo[:, c, cols], b_hi[:, c, :], start=False, stop=(c == chunks - 1))
                return last

            def m_product():
                for o in range(DC):
                    pe.wait_ge(wqk_loaded[o], 32)
                    for c in range(DC):
                        last = pe.matmul(ps[:, W_BANKS[c], :], wk_in[:, o, c * P:(c + 1) * P], wq_in[:, o, :],
                                         start=(o == 0), stop=(o == DC - 1))
                        if o == DC - 1:
                            last.then_inc(m_done, 1)

            def bias_and_wv_products():
                pe.wait_ge(parts_ready, DC)
                pe.wait_ge(bb_part_ready, 1)
                pe.matmul(ps[:, C_BANK, :], ones[:], c_part[:], start=True, stop=True).then_inc(c_done, 1)
                pe.wait_ge(adjt_ready, 1)
                for m in range(DC):
                    pe.matmul(ps[:, U_BANK, m:m + 1], u_part[:, m * P:(m + 1) * P], ones[:, 0:1],
                              start=True, stop=True)
                pe.matmul(ps[:, U_BANK, DC:DC + 1], ones[:], bb_part[:], start=True, stop=True).then_inc(u_done, 1)
                pe.wait_ge(wv_loaded, 16)
                for c in range(DC):
                    pe.wait_ge(m_lo_ready, c + 1)
                    for o in range(DC):
                        last = pe.transpose(ps[:, W_BANKS[c], o * P:(o + 1) * P], wv_in[:, o, c * P:(c + 1) * P],
                                            ident[:])
                    last.then_inc(wvt_done, 1)
                pe.wait_ge(wvt_lo_ready, 2)

            def step(this, prev, main, ahead, older=True):
                if main:
                    pe.wait_ge(ht_lo_ready[1], this)
                    for m in range(DC):
                        cols = slice(m * P, (m + 1) * P)
                        last = product(ps[:, G + m // 2, m % 2 * N:m % 2 * N + N], DC,
                                       (m_hi, m_lo), cols, (ht_hi, ht_lo))
                        if m % 2:
                            last.then_inc(g_done[m // 2], 1)
                    if not prev:
                        pe.wait_ge(wvt_lo_ready, DC)
                    for t in range(NT):
                        if prev and older:
                            pe.wait_ge(y_ready[t], this - 2)
                        cols = slice(t * P, (t + 1) * P)
                        product(ps[:, V + t, :], DC,
                                (ht_hi, ht_lo), cols, (wvt_hi, wvt_lo)).then_inc(v_done[t], 1)
                if prev:
                    pe.wait_ge(hat_lo_ready, this - 1)
                    pe.wait_ge(h1_lo_ready[1], this - 1)
                    for m in range(DC):
                        cols = slice(m * P, (m + 1) * P)
                        last = product(ps[:, Z + m // 2, m % 2 * N:m % 2 * N + N], NT,
                                       (h1_hi, h1_lo), cols, (hat_hi, hat_lo))
                        if m % 2:
                            last.then_inc(z_done[m // 2], 1)
                if main:
                    pe.wait_ge(dn_ready, this)
                    if prev:
                        pe.wait_ge(x1_ready[0], this - 1)
                    for t in range(NT):
                        last = pe.transpose(ps[:, DR, t * P:(t + 1) * P], dn[:, t:t + 1].to_broadcast([P, P]), ident[:])
                    last.then_inc(dr_done, 1)
                    pe.wait_ge(g_lo_ready[1], this)
                    for t in range(NT):
                        cols = slice(t * P, (t + 1) * P)
                        product(ps[:, G + t, 0:N], DC,
                                (g_hi, g_lo), cols, (ht_hi, ht_lo)).then_inc(s_done[t], 1)
                if ahead:
                    if not main:
                        m_product()
                        pe.wait_ge(ident_ready, 1)
                    pe.wait_ge(adj_loaded, (this + 1) * 16)
                    for k in range(NT):
                        for q in range(NT):
                            last = pe.transpose(ps[:, AT, k * N + q * P:k * N + (q + 1) * P],
                                                adj_in[:, q, k * P:(k + 1) * P], ident[:])
                    last.then_inc(at_done, 1)
                    pe.wait_ge(h_ready[0], this + 1)
                    pe.wait_ge(h_ready[1], this + 1)
                    for c in range(DC):
                        if prev and c % 2 == 0:
                            pe.wait_ge(z_lo_ready[c // 2], this - 1)
                        for t in range(NT):
                            last = pe.transpose(ps[:, HT + c // 2, c % 2 * N + t * P:c % 2 * N + (t + 1) * P],
                                                h[:, t, c * P:(c + 1) * P], ident[:])
                        if c % 2:
                            last.then_inc(ht_done[c // 2], 1)
                    if not main:
                        bias_and_wv_products()
                if prev:
                    pe.wait_ge(w_lo_ready, 1)
                    pe.wait_ge(z_lo_ready[1], this - 1)
                    for t in range(NT):
                        if main:
                            pe.wait_ge(v_lo_ready[t], this)
                        cols = slice(t * P, (t + 1) * P)
                        product(ps[:, O1 + t, :], DC,
                                (z_hi, z_lo), cols, (w_hi, w_lo)).then_inc(o1_done[t], 1)
                if main:
                    pe.wait_ge(p_lo_ready[1], this)
                    if not prev:
                        pe.wait_ge(consts_ready, 2)
                    pe.wait_ge(v_lo_ready[1], this)
                    pe.wait_ge(s_sum_ready, this)
                    if ahead:
                        pe.wait_ge(adjt_ready, this + 1)
                    for t in range(NT):
                        if ahead and t:
                            pe.wait_ge(ht_lo_ready[1], this + 1)
                        cols = slice(t * P, (t + 1) * P)
                        for a, width in enumerate((HD + 2, HD)):
                            last = product(ps[:, O[t] + a, 0:width], NT, (p_hi, p_lo), cols,
                                           (v_hi[:, :, a, 0:width], v_lo[:, :, a, 0:width]))
                        last.then_inc(o_done[t], 1)

            steps(pe, step)


_INS = ["x", "adj", "L0_gnn_Wq_w", "L0_gnn_Wq_b", "L0_gnn_Wk_w", "L0_gnn_Wk_b", "L0_gnn_Wv_w", "L0_gnn_Wv_b",
        "L1_gnn_W", "L1_gnn_b"]


def kernel(**inputs):
    import numpy as _np
    import concourse.bacc as _bacc
    from concourse import mybir as _mybir
    from concourse.bass_utils import run_bass_kernel_spmd as _run

    nc = _bacc.Bacc("TRN2", target_bir_lowering=False, num_devices=1)
    arrays, args = {}, []
    for name in _INS:
        a = _np.ascontiguousarray(inputs[name])
        arrays[f"in_{name}_dram"] = a
        args.append(nc.dram_tensor(f"in_{name}_dram", a.shape, _mybir.dt.from_np(a.dtype), kind="ExternalInput").ap())
    out = nc.dram_tensor("out_dram", (B, N, D), _mybir.dt.float32, kind="ExternalOutput").ap()
    gnn_program(nc, *args, out)
    r = _run(nc, [arrays], core_ids=[0])
    return r.results[0]["out_dram"]
```
